# Optimizing a Trainium2 kernel written in Bass

```python
import numpy as np
import jax
import jax.numpy as jnp

def _softmax(x, axis=-1):
    return jax.nn.softmax(x, axis=axis)

def _gelu(x):
    return jax.nn.gelu(x, approximate=True)

def _silu(x):
    return jax.nn.silu(x)

def _sigmoid(x):
    return jax.nn.sigmoid(x)

def _layernorm(x, axis=-1, eps=1e-05):
    m = jnp.mean(x, axis=axis, keepdims=True)
    v = jnp.var(x, axis=axis, keepdims=True)
    return (x - m) / jnp.sqrt(v + eps)

def _scatter_add(tgt, idx, src, axis=0):
    return tgt.at[idx].add(src)

def _segment_sum(src, seg, n):
    return jax.ops.segment_sum(src, seg, n)
kernel_name = 'mk_flamingo_gated_d1_seqx_r4_85418f'

def setup_inputs(seed: int=0):
    np.random.seed(seed)
    _w = jnp.asarray

    def _rec_inputs():
        import jax
        import jax.numpy as jnp
        _rk = jax.random.key(seed)
        x = -0.0003929 + 0.9999 * jax.random.normal(jax.random.fold_in(_rk, 1), (8, 512, 256), jnp.float32)
        _lenS = 512 - jax.random.randint(jax.random.fold_in(_rk, 7), (8,), 0, max(1, 512 // 4) + 1, jnp.int32)
        _lenS2 = 512 - jax.random.randint(jax.random.fold_in(_rk, 8), (8,), 0, max(1, 512 // 4) + 1, jnp.int32)
        _ctx_512P = jax.random.normal(jax.random.fold_in(_rk, 11), (8, 16, 128), jnp.float32)
        _ctx_512c = jax.random.dirichlet(jax.random.fold_in(_rk, 511), 0.3 * jnp.ones((16,), jnp.float32), (8, 512))
        _ctx_512t = jnp.einsum('bsk,bkd->bsd', _ctx_512c, _ctx_512P)
        _ctx_512t = _ctx_512t * jax.lax.rsqrt(jnp.mean(jnp.square(_ctx_512t)) + 1e-12) * 0.953939
        ctx_512 = -1.39393e-06 + 0.999914 * (_ctx_512t + 0.3 * jax.random.normal(jax.random.fold_in(_rk, 611), (8, 512, 128), jnp.float32))
        _g = jax.random.normal(jax.random.fold_in(_rk, 9001), (2, 1), jnp.float32)
        _g = jnp.sign(_g) * jnp.maximum(jnp.abs(_g), 1.0) + (_g == 0) * 1.0
        g_xattn = _g[0]
        g_ffn = _g[1]
        return (x, ctx_512, g_xattn, g_ffn)
    x, ctx_512, g_xattn, g_ffn = _rec_inputs()

    def _L0_xattn_setup():
        import jax, jax.numpy as jnp
        import numpy as np
        HEADS = 16
        D_MODEL = 256
        IMG_MODEL = 128
        D_K = D_MODEL // HEADS
        key = jax.random.key(seed)
        ks = jax.random.split(key, 12)
        B, LQ, LKV = (8, 512, 256)
        s_dm = 1.0 / np.sqrt(D_MODEL)
        s_im = 1.0 / np.sqrt(IMG_MODEL)
        return {'q': jax.random.normal(ks[0], (B, LQ, D_MODEL), jnp.float32), 'k': jax.random.normal(ks[1], (B, LKV, IMG_MODEL), jnp.float32), 'v': jax.random.normal(ks[2], (B, LKV, IMG_MODEL), jnp.float32), 'Wq': jax.random.normal(ks[3], (D_MODEL, D_MODEL), jnp.float32) * s_dm, 'bq': jnp.zeros((D_MODEL,), jnp.float32), 'Wk': jax.random.normal(ks[4], (IMG_MODEL, D_MODEL), jnp.float32) * s_im, 'bk': jnp.zeros((D_MODEL,), jnp.float32), 'Wv': jax.random.normal(ks[5], (IMG_MODEL, D_MODEL), jnp.float32) * s_im, 'bv': jnp.zeros((D_MODEL,), jnp.float32), 'Wo': jax.random.normal(ks[6], (D_MODEL, D_MODEL), jnp.float32) * s_dm, 'bo': jnp.zeros((D_MODEL,), jnp.float32)}
    _L0_xattn_all = _L0_xattn_setup()
    _L0_xattn_in = {k: v for k, v in _L0_xattn_all.items() if k in ('Wq', 'bq', 'Wk', 'bk', 'Wv', 'bv', 'Wo', 'bo')}
    del _L0_xattn_all

    def _L0_ffn_setup():
        import jax, jax.numpy as jnp
        import numpy as np
        D_MODEL = 256
        NUM_HEADS = 4
        NUM_EXPERTS = 8
        TOP_K = 2
        D_FF = 256
        EPS = 1e-06

        def _rmsnorm(x, g):
            return x * jax.lax.rsqrt(jnp.mean(x * x, axis=-1, keepdims=True) + EPS) * g

        def _swiglu(x, w1, w2, w3):
            return jax.nn.silu(x @ w1.T) * (x @ w3.T) @ w2.T
        key = jax.random.key(seed)
        ks = jax.random.split(key, 16)
        d, e, f = (D_MODEL, NUM_EXPERTS, D_FF)
        dc = d // 4
        s = 0.02
        return {'X': jax.random.normal(ks[0], (2, 256, d), dtype=jnp.float32), 'g1': jnp.ones((d,), jnp.float32), 'g2': jnp.ones((d,), jnp.float32), 'Wq': jax.random.normal(ks[1], (d, d), jnp.float32) * s, 'Wkc': jax.random.normal(ks[2], (dc, d), jnp.float32) * s, 'Wvc': jax.random.normal(ks[3], (dc, d), jnp.float32) * s, 'Wo': jax.random.normal(ks[4], (d, d), jnp.float32) * s, 'Wr': jax.random.normal(ks[5], (e, d), jnp.float32) * s, 'expert_bias': jnp.zeros((e,), jnp.float32), 'sW1': jax.random.normal(ks[6], (f, d), jnp.float32) * s, 'sW2': jax.random.normal(ks[7], (d, f), jnp.float32) * s, 'sW3': jax.random.normal(ks[8], (f, d), jnp.float32) * s, 'eW1': jax.random.normal(ks[9], (e, f, d), jnp.float32) * s, 'eW2': jax.random.normal(ks[10], (e, d, f), jnp.float32) * s, 'eW3': jax.random.normal(ks[11], (e, f, d), jnp.float32) * s}
    _L0_ffn_all = _L0_ffn_setup()
    _L0_ffn_in = {k: v for k, v in _L0_ffn_all.items() if k in ('g1', 'g2', 'Wq', 'Wkc', 'Wvc', 'Wo', 'Wr', 'expert_bias', 'sW1', 'sW2', 'sW3', 'eW1', 'eW2', 'eW3')}
    del _L0_ffn_all
    return {'x': x, 'ctx_512': ctx_512, 'g_xattn': g_xattn, 'g_ffn': g_ffn, 'L0_xattn_Wq': _L0_xattn_in['Wq'], 'L0_xattn_bq': _L0_xattn_in['bq'], 'L0_xattn_Wk': _L0_xattn_in['Wk'], 'L0_xattn_bk': _L0_xattn_in['bk'], 'L0_xattn_Wv': _L0_xattn_in['Wv'], 'L0_xattn_bv': _L0_xattn_in['bv'], 'L0_xattn_Wo': _L0_xattn_in['Wo'], 'L0_xattn_bo': _L0_xattn_in['bo'], 'L0_ffn_g1': _L0_ffn_in['g1'], 'L0_ffn_g2': _L0_ffn_in['g2'], 'L0_ffn_Wq': _L0_ffn_in['Wq'], 'L0_ffn_Wkc': _L0_ffn_in['Wkc'], 'L0_ffn_Wvc': _L0_ffn_in['Wvc'], 'L0_ffn_Wo': _L0_ffn_in['Wo'], 'L0_ffn_Wr': _L0_ffn_in['Wr'], 'L0_ffn_expert_bias': _L0_ffn_in['expert_bias'], 'L0_ffn_sW1': _L0_ffn_in['sW1'], 'L0_ffn_sW2': _L0_ffn_in['sW2'], 'L0_ffn_sW3': _L0_ffn_in['sW3'], 'L0_ffn_eW1': _L0_ffn_in['eW1'], 'L0_ffn_eW2': _L0_ffn_in['eW2'], 'L0_ffn_eW3': _L0_ffn_in['eW3']}

def reference(x, ctx_512, g_xattn, g_ffn, L0_xattn_Wq, L0_xattn_bq, L0_xattn_Wk, L0_xattn_bk, L0_xattn_Wv, L0_xattn_bv, L0_xattn_Wo, L0_xattn_bo, L0_ffn_g1, L0_ffn_g2, L0_ffn_Wq, L0_ffn_Wkc, L0_ffn_Wvc, L0_ffn_Wo, L0_ffn_Wr, L0_ffn_expert_bias, L0_ffn_sW1, L0_ffn_sW2, L0_ffn_sW3, L0_ffn_eW1, L0_ffn_eW2, L0_ffn_eW3):
    import jax
    import jax.numpy as jnp

    def _L0_xattn_ref(q, k, v, Wq, bq, Wk, bk, Wv, bv, Wo, bo):
        import jax, jax.numpy as jnp
        import numpy as np
        HEADS = 16
        D_MODEL = 256
        IMG_MODEL = 128
        D_K = D_MODEL // HEADS
        B, LQ, _ = q.shape
        LKV = k.shape[1]
        qh = (q @ Wq + bq).reshape(B, LQ, HEADS, D_K).transpose(0, 2, 1, 3)
        kh = (k @ Wk + bk).reshape(B, LKV, HEADS, D_K).transpose(0, 2, 1, 3)
        vh = (v @ Wv + bv).reshape(B, LKV, HEADS, D_K).transpose(0, 2, 1, 3)
        scale = 1.0 / np.sqrt(D_K)
        scores = jnp.einsum('bhqd,bhkd->bhqk', qh, kh) * scale
        attn = jax.nn.softmax(scores, axis=-1)
        out = jnp.einsum('bhqk,bhkd->bhqd', attn, vh)
        concat = out.transpose(0, 2, 1, 3).reshape(B, LQ, D_MODEL)
        return concat @ Wo + bo

    def _L0_ffn_ref(X, g1, g2, Wq, Wkc, Wvc, Wo, Wr, expert_bias, sW1, sW2, sW3, eW1, eW2, eW3):
        import jax, jax.numpy as jnp
        import numpy as np
        D_MODEL = 256
        NUM_HEADS = 4
        NUM_EXPERTS = 8
        TOP_K = 2
        D_FF = 256
        EPS = 1e-06

        def _rmsnorm(x, g):
            return x * jax.lax.rsqrt(jnp.mean(x * x, axis=-1, keepdims=True) + EPS) * g

        def _swiglu(x, w1, w2, w3):
            return jax.nn.silu(x @ w1.T) * (x @ w3.T) @ w2.T
        B, S, d = X.shape
        H = NUM_HEADS
        dk = d // H
        scale = 1.0 / jnp.sqrt(jnp.float32(dk))
        nx = _rmsnorm(X, g1)
        Q = (nx @ Wq.T).reshape(B, S, H, dk).transpose(0, 2, 1, 3)
        Kc = nx @ Wkc.T
        Vc = nx @ Wvc.T
        scores = jnp.einsum('bhsd,btd->bhst', Q, Kc) * scale
        attn = jax.nn.softmax(scores, axis=-1)
        out = jnp.einsum('bhst,btd->bhsd', attn, Vc)
        out = out.transpose(0, 2, 1, 3).reshape(B, S, d) @ Wo.T
        X = X + out
        nx = _rmsnorm(X, g2)
        xf = nx.reshape(-1, d)
        logits = xf @ Wr.T + expert_bias
        rw = jax.nn.softmax(logits, axis=-1)
        topw, topi = jax.lax.top_k(rw, TOP_K)
        topw = jax.nn.softmax(topw, axis=-1)
        combine = jnp.sum(jax.nn.one_hot(topi, NUM_EXPERTS, dtype=xf.dtype) * topw[..., None], axis=1)
        shared = _swiglu(xf, sW1, sW2, sW3)
        h = jax.nn.silu(jnp.einsum('td,efd->etf', xf, eW1)) * jnp.einsum('td,efd->etf', xf, eW3)
        eo = jnp.einsum('etf,edf->etd', h, eW2)
        specialist = jnp.einsum('te,etd->td', combine, eo)
        moe_out = (shared + specialist).reshape(B, S, d)
        return X + moe_out
    x = x + jnp.tanh(g_xattn[0]) * _L0_xattn_ref(_layernorm(x, axis=-1), ctx_512, ctx_512, L0_xattn_Wq, L0_xattn_bq, L0_xattn_Wk, L0_xattn_bk, L0_xattn_Wv, L0_xattn_bv, L0_xattn_Wo, L0_xattn_bo)
    x = x + jnp.tanh(g_ffn[0]) * _L0_ffn_ref(_layernorm(x, axis=-1), L0_ffn_g1, L0_ffn_g2, L0_ffn_Wq, L0_ffn_Wkc, L0_ffn_Wvc, L0_ffn_Wo, L0_ffn_Wr, L0_ffn_expert_bias, L0_ffn_sW1, L0_ffn_sW2, L0_ffn_sW3, L0_ffn_eW1, L0_ffn_eW2, L0_ffn_eW3)
    return x

_drawn_inputs = setup_inputs


def setup_inputs(seed=0):
    import zlib

    import numpy as np

    out = dict(_drawn_inputs(seed))
    spreads = {'L0_xattn_bq': (0.0, 0.359),
     'L0_xattn_bk': (0.0, 0.8),
     'L0_xattn_bv': (0.0, 0.1),
     'L0_xattn_bo': (0.0, 0.1),
     'L0_ffn_g1': (1.0, 0.2),
     'L0_ffn_g2': (1.0, 0.2),
     'L0_ffn_expert_bias': (0.0, 0.1)}
    factors = {'L0_ffn_Wq': 8.0, 'L0_ffn_Wkc': 8.0}
    for name, (base, spread) in spreads.items():
        noise = np.random.default_rng([zlib.crc32(name.encode()), seed]).standard_normal(out[name].shape)
        drawn = base * np.exp(spread * noise) if base else spread * noise
        out[name] = jnp.asarray(drawn.astype(out[name].dtype))
    for name, factor in factors.items():
        out[name] = (out[name] * factor).astype(out[name].dtype)
    return out
```

```python
from contextlib import ExitStack

import concourse.bass as bass
from concourse import mybir

F32 = mybir.dt.float32
F32R = mybir.dt.float32r
U32 = mybir.dt.uint32
ALU = mybir.AluOpType
ACT = mybir.ActivationFunctionType
AX = mybir.AxisListType

B = 8
T = 512
D = 256
C = 128
P = 128
QT = T // P
DH = D // P
HEADS = 16
DK = D // HEADS
PACKS = 4
HP = HEADS // PACKS
SLABS = HEADS // 2
LN_EPS = 1e-5
RMS_EPS = 1e-6


def cross_attention(nc, x, ctxT, g_xattn, wq, bq, wk, bk, wv, bv, wo, bo, identity, key_rows, x1):
    with ExitStack() as ctx:
        def sb(name, shape, dt=F32):
            return ctx.enter_context(nc.sbuf_tensor("xa_" + name, shape, dt))

        def psum(name, shape):
            return ctx.enter_context(nc.psum_tensor("xa_" + name, shape, F32))

        def sem(name):
            return ctx.enter_context(nc.semaphore("xa_" + name))

        ident = sb("ident", [P, P])
        wq_sb = sb("wq", [P, DH, D])
        wk_sb = sb("wk", [P, D])
        wv_sb = sb("wv", [P, D])
        wo_sb = sb("wo", [P, DH, D])
        bq_sb = sb("bq", [P, DH])
        bk_sb = sb("bk", [P, DH])
        bv_sb = sb("bv", [P, D])
        bo_sb = sb("bo", [P, D])
        gate = sb("gate", [P, 1])
        gated_bo = sb("gated_bo", [P, D])
        tick = sb("tick", [P, 16])
        veps_tick = sb("veps_tick", [P, 1])
        neg_half = sb("neg_half", [P, QT])
        key_init = sb("key_init", [P, 2, T])

        xt = sb("xt", [P, QT, D])
        ctx_sb = sb("ctx", [P, T])
        stats = sb("stats", [P, QT, 6])
        mv = sb("mv", [P, QT, 2])
        veps = sb("veps", [P, QT])
        rstd = sb("rstd", [P, QT])
        xn = sb("xn", [P, QT, D])
        xnT = sb("xnT", [P, DH, T])
        q_hi = sb("q_hi", [P, DH, T], F32R)
        q_lo = sb("q_lo", [P, DH, T], F32R)
        k_hi = sb("k_hi", [P, DH, T], F32R)
        k_lo = sb("k_lo", [P, DH, T], F32R)
        v_new = sb("v_new", [P, QT, D])
        v_aug = sb("v_aug", [P, QT, HEADS, 2 * DK])
        q_slab = sb("q_slab", [P, SLABS, T], F32R)
        k_slab = sb("k_slab", [P, HEADS, T], F32R)
        q_words = q_slab[:, :, :].bitcast(F32)
        k_words = k_slab[:, :, :].bitcast(F32)
        row_max = sb("row_max", [P, 2, QT, HP])
        m_hi = sb("m_hi", [HP, T], F32R)
        m_lo = sb("m_lo", [HP, T], F32R)
        probs = sb("probs", [P, 4, 2, T])
        o_pack = sb("o_pack", [P, PACKS, T])
        r_sum = sb("r_sum", [P, QT, HEADS])
        o_tok = sb("o_tok", [P, QT, D])
        oT = sb("oT", [P, DH, T])
        x_res = sb("x_res", [P, QT, D])
        x_bias = sb("x_bias", [P, QT, D])
        x1_sb = sb("x1_sb", [P, QT, D])

        ps_s = psum("ps_s", [P, 2, T])
        ps_t = psum("ps_t", [P, 2, 2, T])
        ps_o = psum("ps_o", [P, T])
        ps_m = psum("ps_m", [P, T])

        consts = sem("consts")
        gp_set = sem("gp_set")
        gate_ready = sem("gate_ready")
        gbo_ready = sem("gbo_ready")
        slabs_set = sem("slabs_set")
        x_loaded = sem("x_loaded")
        ctx_loaded = sem("ctx_loaded")
        xres_loaded = sem("xres_loaded")
        stat_done = sem("stat_done")
        mv_done = sem("mv_done")
        rstd_step = sem("rstd_step")
        xn_ready = sem("xn_ready")
        xT_turned = sem("xT_turned")
        xT_copied = sem("xT_copied")
        q_done = sem("q_done")
        q_hi_ready = sem("q_hi_ready")
        q_lo_ready = sem("q_lo_ready")
        k_done = sem("k_done")
        k_hi_ready = sem("k_hi_ready")
        k_lo_ready = sem("k_lo_ready")
        v_done = sem("v_done")
        v_new_ready = sem("v_new_ready")
        v_ready = sem("v_ready")
        pack_loaded = [sem(f"pack_loaded{p}") for p in range(PACKS)]
        s_ready = sem("s_ready")
        max_done = sem("max_done")
        m_turned = sem("m_turned")
        m_hi_ready = sem("m_hi_ready")
        m_lo_ready = sem("m_lo_ready")
        m_loaded = [sem(f"m_loaded{i}") for i in range(2)]
        st_ready = sem("st_ready")
        exp_done = sem("exp_done")
        pv_done = sem("pv_done")
        o_copied = sem("o_copied")
        o_turned = sem("o_turned")
        r_done = sem("r_done")
        o_normed = sem("o_normed")
        oT_turned = sem("oT_turned")
        oT_copied = sem("oT_copied")
        out_done = sem("out_done")
        xbias_ready = sem("xbias_ready")
        x1_ready = sem("x1_ready")
        x1_stored = sem("x1_stored")

        x_v = x.rearrange("b (t p) d -> b p t d", p=P)
        x1_v = x1.rearrange("b (t p) d -> b p t d", p=P)

        def one(ap, b):
            return ap[bass.ds(b, 1)].rearrange("o p t d -> p (o t) d")

        PACK_LOAD = 9 * 16
        MAX_LOAD = 4 * 16
        TASKS = {(0, "A"): [("m", 0)], (0, "B"): [("O", 0)], (1, "A"): [("O", 1)], (1, "B"): [("O", 2)],
                 (2, "A"): [("O", 3)], (2, "B"): [("K", 0)], (3, "A"): [("X", 0)], (3, "B"): [("X", 1)],
                 (4, "A"): [("m", 1)], (4, "B"): [("Q", 0)], (5, "A"): [("K", 1)], (5, "B"): [("Q", 1)],
                 (6, "A"): [("T", 0)], (6, "B"): [("T", 1)], (7, "A"): [("W", 0)], (7, "B"): [("W", 1)],
                 (8, "A"): [("m", 2)], (8, "B"): [("V", 0)], (9, "A"): [("V", 1)], (12, "A"): [("m", 3)]}
        FRONT, TAIL = "XKQV", "OTW"

        def tasks(b, k, place, first, last):
            for kind, i in TASKS.get((k, place), []):
                if kind in FRONT and not last:
                    yield kind, i, b + 1
                elif kind in TAIL and not first:
                    yield kind, i, b - 1
                elif kind == "m" and not (last and i == 3):
                    yield kind, i, 4 * b + i + 1

        def freed(kind, i, b):
            return {"X": [(xT_copied, 2 * b + i + 1)], "K": [(k_hi_ready, 2 * b + i + 1), (k_lo_ready, 2 * b + i + 1)],
                    "Q": [(q_hi_ready, 2 * b + i + 1), (q_lo_ready, 2 * b + i + 1)], "V": [(v_new_ready, 2 * b + i + 1)],
                    "O": [(o_normed, 4 * b + i + 1)], "T": [(oT_copied, 2 * b + i + 1)], "W": [(x1_ready, 2 * b + i + 1)],
                    "m": [(m_hi_ready, b + 1), (m_lo_ready, b + 1)]}[kind]

        def before(b, k, place, first, last):
            places = [(kk, pl) for kk in range(16) for pl in "AB" if (kk, pl) in TASKS]
            at = places.index((k, place))
            for kk, pl in reversed(places[:at]):
                for t in tasks(b, kk, pl, first, last):
                    return t
            return "m", 3, 4 * b

        block = ctx.enter_context(nc.Block())

        @block.sync
        def _(sp):
            for dst, src in ((ident, identity), (wk_sb, wk), (wv_sb, wv)):
                sp.dma_start(dst[:, :], src).then_inc(consts, 16)
            sp.dma_start(key_init[:, :, :], key_rows).then_inc(consts, 16)
            for dst, src in ((wq_sb, wq), (wo_sb, wo)):
                sp.dma_start(dst[:, :, :], src.rearrange("(h p) n -> p h n", p=P)).then_inc(consts, 16)
            for dst, src in ((bq_sb, bq), (bk_sb, bk)):
                sp.dma_start(dst[:, :], src).then_inc(consts, 16)
            for dst, src in ((bv_sb, bv), (bo_sb, bo), (gate, g_xattn)):
                sp.dma_start(dst[:, :], src.partition_broadcast(P)).then_inc(consts, 16)

            def load_x(b, first=False):
                if not first:
                    sp.wait_ge(xn_ready, QT * b)
                sp.dma_start(xt[:, :, :], one(x_v, b)).then_inc(x_loaded, 16)
                if not first:
                    sp.wait_ge(v_done, 2 * b)
                sp.dma_start(ctx_sb[:, :], ctxT[bass.ds(b, 1)].rearrange("o p t -> p (o t)")).then_inc(ctx_loaded, 16)

            def load_pack(b, p, first=False):
                if first and p == 0:
                    sp.wait_ge(slabs_set, 3)
                if p == 0:
                    for split in (k_hi_ready, k_lo_ready, q_hi_ready, q_lo_ready):
                        sp.wait_ge(split, 2 * b + 2)
                if not first:
                    sp.wait_ge(st_ready, 32 * b - 32 + 8 * p + 8)
                for r, (qs, ks) in enumerate(((q_hi, k_hi), (q_hi, k_lo), (q_lo, k_hi))):
                    sp.dma_start(q_words[32 * r:32 * r + 32, 2 * p:2 * p + 2, :], qs[32 * p:32 * p + 32, :, :].bitcast(F32))\
                      .then_inc(pack_loaded[p], 16)
                    for a in range(2):
                        lo = 32 * p + DK * a
                        sp.dma_start(k_words[32 * r + DK * a:32 * r + DK * a + DK, HP * p + a:HP * p + HP:2, :],
                                     ks[lo:lo + DK, :, :].bitcast(F32)).then_inc(pack_loaded[p], 16)

            def load_max(n, p, first=False):
                sp.wait_ge(m_hi_ready, n + 1)
                sp.wait_ge(m_lo_ready, n + 1)
                if not first:
                    sp.wait_ge(st_ready, 8 * n - 24)
                for r, m in ((96, m_hi), (98, m_lo)):
                    for i in range(2):
                        sp.dma_start(q_words[r:r + 2, 2 * p + i, :], m[2 * i:2 * i + 2, :].bitcast(F32))\
                          .then_inc(m_loaded[p % 2], 16)

            def body(b, first=False, last=False):
                if not last:
                    load_x(b + 1)
                load_max(4 * b + 1, 1, first)
                if not first:
                    load_pack(b, 3)
                    sp.wait_ge(xbias_ready, b - 1)
                    sp.dma_start(x_res[:, :, :], one(x_v, b - 1)).then_inc(xres_loaded, 16)
                load_max(4 * b + 2, 2, first)
                if not last:
                    load_pack(b + 1, 0)
                if not first:
                    sp.wait_ge(x1_ready, 2 * b)
                    sp.dma_start(one(x1_v, b - 1), x1_sb[:, :, :]).then_inc(x1_stored, 16)
                load_max(4 * b + 3, 3, first)
                if not last:
                    load_pack(b + 1, 1)
                    load_max(4 * b + 4, 0)
                    load_pack(b + 1, 2)

            load_x(0, True)
            for p in range(PACKS):
                load_pack(0, p, True)
            load_max(0, 0, True)
            body(0, first=True)
            with sp.Fori(1, B - 1) as b:
                body(b)
            body(B - 1, last=True)
            sp.wait_ge(xbias_ready, B - 1)
            sp.dma_start(x_res[:, :, :], one(x_v, B - 1)).then_inc(xres_loaded, 16)
            sp.wait_ge(x1_ready, 2 * B)
            sp.dma_start(one(x1_v, B - 1), x1_sb[:, :, :]).then_inc(x1_stored, 16)
            sp.wait_ge(x1_stored, 16 * B)

        @block.gpsimd
        def _(pool):
            pool.memset(neg_half[:, :], -0.5).then_inc(gp_set, 1)
            pool.memset(v_aug[:, :, :, :], 1.0).then_inc(gp_set, 1)
            pool.memset(tick[:, :], 0.0).then_inc(gp_set, 1)
            pool.wait_ge(gp_set, 3)

            def bear_wait(n):
                pool.tensor_tensor(tick[:, n:n + 1], tick[:, 0:1], tick[:, 0:1], ALU.add)

            def normalize(b, first=False):
                pool.wait_ge(mv_done, QT * b + QT)
                bear_wait(1)
                pool.tensor_scalar(veps[:, :], mv[:, :, 1], LN_EPS, None, ALU.add).then_inc(rstd_step, 1)
                pool.wait_ge(rstd_step, 2 * b + 1)
                pool.tensor_tensor(rstd[:, :], veps[:, :], neg_half[:, :], ALU.pow).then_inc(rstd_step, 1)
                pool.wait_ge(rstd_step, 2 * b + 2)
                if not first:
                    pool.wait_ge(xT_turned, 2 * b)
                bear_wait(2)
                for t in range(QT):
                    pool.tensor_scalar(xn[:, t, :], xt[:, t, :], mv[:, t, 0:1], rstd[:, t:t + 1],
                                       ALU.subtract, ALU.mult).then_inc(xn_ready, 1)

            def add_bias(b):
                pool.wait_ge(xres_loaded, 16 * b + 16)
                pool.wait_ge(x1_ready, 2 * b)
                for t in range(QT):
                    ins = pool.tensor_tensor(x_bias[:, t, :], x_res[:, t, :], gated_bo[:, :], ALU.add)
                ins.then_inc(xbias_ready, 1)

            def place_v(b, c, first=False):
                pool.wait_ge(v_new_ready, 2 * b + c // 2 + 1)
                if not first:
                    pool.wait_ge(pv_done, 16 * b - 3 + c)
                bear_wait(3 + c)
                pool.tensor_copy(v_aug[:, c, :, 0:DK],
                                 v_new[:, c, :].rearrange("p (h d) -> p h d", d=DK)).then_inc(v_ready, 1)

            def body(b, first=False, last=False):
                if not last:
                    normalize(b + 1)
                if not first:
                    add_bias(b - 1)
                if not last:
                    for c in range(QT):
                        place_v(b + 1, c)

            pool.wait_ge(gbo_ready, 1)
            normalize(0, True)
            for c in range(QT):
                place_v(0, c, True)
            body(0, first=True)
            with pool.Fori(1, B - 1) as b:
                body(b)
            body(B - 1, last=True)
            add_bias(B - 1)

        @block.scalar
        def _(act):
            act.wait_ge(consts, 16 * 11)
            act.activation(gate[:, :], gate[:, :], ACT.Tanh).then_inc(gate_ready, 1)

            def task(kind, i, b, first=False):
                if kind == "X":
                    act.wait_ge(xT_turned, 2 * b + i + 1)
                    act.copy(xnT[:, i, :], ps_m[:, :]).then_inc(xT_copied, 1)
                elif kind in "QK":
                    done, hi, bias, ready = ((q_done, q_hi, bq_sb, q_hi_ready), (k_done, k_hi, bk_sb, k_hi_ready))[kind == "K"]
                    act.wait_ge(done, 2 * b + i + 1)
                    if not first:
                        for p in range(PACKS):
                            act.wait_ge(pack_loaded[p], PACK_LOAD * b)
                    act.activation(hi[:, i, :], ps_m[:, :], ACT.Identity, bias=bias[:, i:i + 1]).then_inc(ready, 1)
                elif kind == "m":
                    act.wait_ge(m_turned, b + 1)
                    if not first:
                        act.wait_ge(m_loaded[i % 2], MAX_LOAD * ((b - i - 1) // 2 + i // 2 + 1))
                    act.mul(m_hi[:, :], ps_m[0:HP, :], -1.0).then_inc(m_hi_ready, 1)
                elif kind == "T":
                    act.wait_ge(oT_turned, 2 * b + i + 1)
                    act.copy(oT[:, i, :], ps_m[:, :]).then_inc(oT_copied, 1)

            def exp(b, k, half, first=False):
                i = 2 * k + half
                act.wait_ge(st_ready, 32 * b + i + 1)
                if not (first and i < 4):
                    act.wait_ge(pv_done, 16 * b + i // 2 - 1)
                act.activation(probs[:, i % 4, :, :], ps_t[:, half, :, :], ACT.Exp, scale=DK ** -0.5)\
                   .then_inc(exp_done, 1)

            def copy_o(b, p, first=False):
                act.wait_ge(pv_done, 16 * b + 4 * p + 4)
                if not first:
                    act.wait_ge(o_turned, 4 * b)
                act.copy(o_pack[:, p, :], ps_o[:, :]).then_inc(o_copied, 1)

            def body(b, first=False, last=False):
                for k in range(16):
                    for t in tasks(b, k, "A", first, last):
                        task(*t)
                    exp(b, k, 0, first)
                    exp(b, k, 1, first)
                    if k % 4 == 0 and k > 0:
                        copy_o(b, k // 4 - 1, first)
                    if k == 0 and not first:
                        copy_o(b - 1, 3, True)
                    for t in tasks(b, k, "B", first, last):
                        task(*t)

            for i in range(2):
                task("X", i, 0)
            for i in range(2):
                task("K", i, 0, True)
                task("Q", i, 0, True)
            task("m", 0, 0, True)
            body(0, first=True)
            with act.Fori(1, B - 1) as b:
                body(b)
            body(B - 1, last=True)
            copy_o(B - 1, 3, True)
            for i in range(2):
                task("T", i, B - 1)

        @block.vector
        def _(dve):
            dve.wait_ge(consts, 16 * 11)
            dve.tensor_copy(q_slab[:, :, :], key_init[:, 0:1, :].broadcast_to([P, SLABS, T])).then_inc(slabs_set, 1)
            for a in range(2):
                dve.tensor_copy(k_slab[:, a::2, :], key_init[:, a:a + 1, :].broadcast_to([P, HEADS // 2, T]))\
                   .then_inc(slabs_set, 1)
            dve.wait_ge(gate_ready, 1)
            dve.tensor_scalar(gated_bo[:, :], bo_sb[:, :], gate[:, 0:1], None, ALU.mult).then_inc(gbo_ready, 1)

            def statistics(b, first=False):
                dve.wait_ge(x_loaded, 16 * b + 16)
                if not first:
                    dve.wait_ge(xn_ready, QT * b)
                for t in range(QT):
                    dve.bn_stats(stats[:, t, :], xt[:, t, :]).then_inc(stat_done, 1)
                dve.wait_ge(stat_done, QT * b + QT)
                dve.tensor_copy(veps_tick[:, 0:1], stats[:, 0, 0:1])
                for t in range(QT):
                    dve.bn_aggr(mv[:, t, :], stats[:, t, :]).then_inc(mv_done, 1)

            def task(kind, i, b, first=False):
                if kind in "QK":
                    done, hi, lo, bias, h_ready, l_ready = (
                        (q_done, q_hi, q_lo, bq_sb, q_hi_ready, q_lo_ready),
                        (k_done, k_hi, k_lo, bk_sb, k_hi_ready, k_lo_ready))[kind == "K"]
                    dve.wait_ge(h_ready, 2 * b + i + 1)
                    dve.scalar_tensor_tensor(out=lo[:, i, :], in0=ps_m[:, :], scalar=bias[:, i:i + 1],
                                             in1=hi[:, i, :].bitcast(F32), op0=ALU.add, op1=ALU.subtract)\
                       .then_inc(l_ready, 1)
                elif kind == "m":
                    dve.wait_ge(m_hi_ready, b + 1)
                    dve.scalar_tensor_tensor(out=m_lo[:, :], in0=ps_m[0:HP, :], scalar=-1.0,
                                             in1=m_hi[:, :].bitcast(F32), op0=ALU.mult, op1=ALU.subtract)\
                       .then_inc(m_lo_ready, 1)
                elif kind == "V":
                    dve.wait_ge(v_done, 2 * b + i + 1)
                    if not first:
                        dve.wait_ge(v_ready, QT * b)
                    dve.tensor_tensor(v_new[:, 2 * i:2 * i + 2, :], ps_m[:, :].rearrange("p (t d) -> p t d", d=D),
                                      bv_sb[:, :].unsqueeze(1).broadcast_to([P, 2, D]), ALU.add).then_inc(v_new_ready, 1)
                elif kind == "O":
                    o = ps_m[:, :].rearrange("p (h e) -> p h e", e=2 * DK)
                    dve.wait_ge(o_turned, 4 * b + i + 1)
                    dve.reciprocal(r_sum[:, i, :], o[:, :, DK]).then_inc(r_done, 1)
                    dve.wait_ge(r_done, 4 * b + i + 1)
                    dve.tensor_tensor(o_tok[:, i, :].rearrange("p (h d) -> p h d", d=DK), o[:, :, 0:DK],
                                      r_sum[:, i, :].unsqueeze(2).broadcast_to([P, HEADS, DK]), ALU.mult)\
                       .then_inc(o_normed, 1)
                elif kind == "W":
                    dve.wait_ge(out_done, 2 * b + i + 1)
                    dve.wait_ge(xbias_ready, b + 1)
                    dve.wait_ge(x1_stored, 16 * b)
                    dve.scalar_tensor_tensor(out=x1_sb[:, 2 * i:2 * i + 2, :].rearrange("p t d -> p (t d)"), in0=ps_m[:, :],
                                             scalar=gate[:, 0:1],
                                             in1=x_bias[:, 2 * i:2 * i + 2, :].rearrange("p t d -> p (t d)"),
                                             op0=ALU.mult, op1=ALU.add).then_inc(x1_ready, 1)

            def row_maximum(n, par, c, t, first=False):
                i = 4 * c + t
                dve.wait_ge(s_ready, 16 * n + i + 1)
                if i == 0 and not first:
                    dve.wait_ge(m_turned, n - 1)
                dve.tensor_reduce(row_max[:, par, t, c:c + 1], ps_s[:, i % 2, :], AX.X, ALU.max).then_inc(max_done, 1)

            def body(b, first=False, last=False):
                for k in range(16):
                    p, c = k // 4, k % 4
                    if k == 1 and not last:
                        statistics(b + 1)
                    scores = not (last and p >= 2)
                    for t in range(2 * scores):
                        row_maximum(4 * b + p + 2, p % 2, c, t)
                    for t in tasks(b, k, "A", first, last):
                        task(*t)
                    for t in range(2, 2 + 2 * scores):
                        row_maximum(4 * b + p + 2, p % 2, c, t)
                    for t in tasks(b, k, "B", first, last):
                        task(*t)

            statistics(0, True)
            for i in range(2):
                task("K", i, 0)
                task("Q", i, 0)
            for i in range(2):
                task("V", i, 0, True)
            for n in range(2):
                for c in range(HP):
                    for t in range(QT):
                        row_maximum(n, n, c, t, True)
                if n == 0:
                    task("m", 0, 0)
            body(0, first=True)
            with dve.Fori(1, B - 1) as b:
                body(b)
            body(B - 1, last=True)
            for i in range(QT):
                task("O", i, B - 1)
            for i in range(2):
                task("W", i, B - 1)

        @block.tensor
        def _(pe):
            pe.wait_ge(consts, 16 * 11)

            def task(kind, i, b, prev):
                if prev is not None:
                    for s, v in freed(*prev):
                        pe.wait_ge(s, v)
                if kind == "X":
                    if i == 0:
                        pe.wait_ge(xn_ready, QT * b + QT)
                    for t in range(QT):
                        mm = pe.transpose(ps_m[:, t * P:(t + 1) * P], xn[:, t, i * P:(i + 1) * P], ident[:, :])
                    mm.then_inc(xT_turned, 1)
                elif kind == "Q":
                    pe.wait_ge(xT_copied, 2 * b + 2)
                    for h in range(DH):
                        mm = pe.matmul(ps_m[:, :], wq_sb[:, h, i * P:(i + 1) * P], xnT[:, h, :],
                                       start=(h == 0), stop=(h == DH - 1))
                    mm.then_inc(q_done, 1)
                elif kind == "K":
                    pe.wait_ge(ctx_loaded, 16 * b + 16)
                    pe.matmul(ps_m[:, :], wk_sb[:, i * P:(i + 1) * P], ctx_sb[:, :], start=True, stop=True)\
                      .then_inc(k_done, 1)
                elif kind == "V":
                    for t in range(2 * i, 2 * i + 2):
                        mm = pe.matmul(ps_m[:, (t % 2) * D:(t % 2 + 1) * D], ctx_sb[:, t * P:(t + 1) * P], wv_sb[:, :],
                                       start=True, stop=True)
                    mm.then_inc(v_done, 1)
                elif kind == "m":
                    pe.wait_ge(max_done, 16 * b + 16)
                    for t in range(QT):
                        mm = pe.transpose(ps_m[0:HP, t * P:(t + 1) * P], row_max[:, i % 2, t, :], ident[:, :])
                    mm.then_inc(m_turned, 1)
                elif kind == "O":
                    pe.wait_ge(o_copied, 4 * b + 4)
                    for p in range(PACKS):
                        mm = pe.transpose(ps_m[:, p * P:(p + 1) * P], o_pack[:, p, i * P:(i + 1) * P], ident[:, :])
                    mm.then_inc(o_turned, 1)
                elif kind == "T":
                    if i == 0:
                        pe.wait_ge(o_normed, 4 * b + 4)
                    for t in range(QT):
                        mm = pe.transpose(ps_m[:, t * P:(t + 1) * P], o_tok[:, t, i * P:(i + 1) * P], ident[:, :])
                    mm.then_inc(oT_turned, 1)
                elif kind == "W":
                    if i == 0:
                        pe.wait_ge(oT_copied, 2 * b + 2)
                    for t in range(2 * i, 2 * i + 2):
                        for h in range(DH):
                            mm = pe.matmul(ps_m[:, (t % 2) * D:(t % 2 + 1) * D], oT[:, h, t * P:(t + 1) * P],
                                           wo_sb[:, h, :], start=(h == 0), stop=(h == DH - 1))
                    mm.then_inc(out_done, 1)

            def max_scores(n, p, c, t, b, first=False):
                i = 4 * c + t
                if i == 0:
                    pe.wait_ge(pack_loaded[p], PACK_LOAD * (b + 1))
                if not (first and i < 2):
                    pe.wait_ge(max_done, 16 * n + i - 1)
                pe.matmul(ps_s[:, i % 2, :], q_slab[0:96, 2 * p + c // 2, t * P:(t + 1) * P],
                          k_slab[0:96, HP * p + c, :], start=True, stop=True).then_inc(s_ready, 1)

            def exp_scores(b, p, c, half, first=False):
                i = 8 * p + 2 * c + half
                if c == 0 and half == 0:
                    pe.wait_ge(m_loaded[p % 2], MAX_LOAD * (2 * b + p // 2 + 1))
                if not (first and i < 2):
                    pe.wait_ge(exp_done, 32 * b + i - 1)
                for j in range(2):
                    h = 2 * half + j
                    mm = pe.matmul(ps_t[:, half, j, :], k_slab[0:100, HP * p + h, c * P:(c + 1) * P],
                                   q_slab[0:100, 2 * p + half, :], start=True, stop=True)
                mm.then_inc(st_ready, 1)

            def weigh_values(b, k, first=False):
                p, c = k // 4, k % 4
                pe.wait_ge(exp_done, 32 * b + 2 * k + 2)
                if p == 0:
                    pe.wait_ge(v_ready, QT * b + c + 1)
                if c == 0 and not (first and p == 0):
                    pe.wait_ge(o_copied, 4 * b + p)
                for j in range(HP):
                    mm = pe.matmul(ps_o[32 * j:32 * j + 32, :], v_aug[:, c, HP * p + j, :],
                                   probs[:, (2 * k + j // 2) % 4, j % 2, :], start=(c == 0), stop=(c == QT - 1),
                                   skip_group_check=True)
                mm.then_inc(pv_done, 1)

            def body(b, first=False, last=False):
                for k in range(16):
                    p, c = k // 4, k % 4
                    n, sp_, sb_ = 4 * b + p + 2, (p + 2) % PACKS, b + (p + 2) // PACKS
                    scores = not (last and p >= 2)
                    if scores:
                        max_scores(n, sp_, c, 0, sb_)
                    if scores:
                        max_scores(n, sp_, c, 1, sb_)
                    for t in tasks(b, k, "A", first, last):
                        kind, i, bb = t
                        task(kind, (i + 1) % 4 if kind == "m" else i, bb, before(b, k, "A", first, last))
                    exp_scores(b, p, c, 0, first)
                    if scores:
                        max_scores(n, sp_, c, 2, sb_)
                    exp_scores(b, p, c, 1, first)
                    if scores:
                        max_scores(n, sp_, c, 3, sb_)
                    if k > 0:
                        weigh_values(b, k - 1, first)
                    elif not first:
                        weigh_values(b - 1, 15)
                    for t in tasks(b, k, "B", first, last):
                        kind, i, bb = t
                        task(kind, i, bb, before(b, k, "B", first, last))

            task("X", 0, 0, None)
            task("X", 1, 0, ("X", 0, 0))
            task("K", 0, 0, ("X", 1, 0))
            task("Q", 0, 0, ("K", 0, 0))
            task("K", 1, 0, ("Q", 0, 0))
            task("Q", 1, 0, ("K", 1, 0))
            task("V", 0, 0, ("Q", 1, 0))
            task("V", 1, 0, ("V", 0, 0))
            for n in range(2):
                for c in range(HP):
                    for t in range(QT):
                        max_scores(n, n, c, t, 0, n == 0)
                if n == 0:
                    task("m", 0, 0, ("V", 1, 0))
            body(0, first=True)
            with pe.Fori(1, B - 1) as b:
                body(b)
            body(B - 1, last=True)
            weigh_values(B - 1, 15)
            prev = ("m", 2, 4 * (B - 1) + 3)
            for kind, i in [("O", i) for i in range(QT)] + [("T", i) for i in range(2)] + [("W", i) for i in range(2)]:
                task(kind, i, B - 1, prev)
                prev = (kind, i, B - 1)


KC = D // 4
H2 = D // KC


def self_attention(nc, x1, g_ffn, g1, wqT, wkvT, woT, g2, identity, key_rows, x_norm, base, x_moe):
    with ExitStack() as ctx:
        def sb(name, shape, dt=F32):
            return ctx.enter_context(nc.sbuf_tensor("sa_" + name, shape, dt))

        def psum(name, shape):
            return ctx.enter_context(nc.psum_tensor("sa_" + name, shape, F32))

        def sem(name):
            return ctx.enter_context(nc.semaphore("sa_" + name))

        ident = sb("ident", [P, P])
        wq_sb = sb("wq", [P, DH, D])
        wkv_sb = sb("wkv", [P, DH, 2 * KC])
        wo_sb = sb("wo", [P, DH, D])
        g1_sb = sb("g1", [P, DH])
        g2_sb = sb("g2", [P, DH])
        gate = sb("gate", [P, 1])
        tick = sb("tick", [P, 16])
        veps_tick = sb("veps_tick", [P, 1])
        neg_half = sb("neg_half", [P, QT])
        ones = sb("ones", [P, 32])
        key_init = sb("key_init", [P, 2, T])

        xt = sb("xt", [P, QT, D])
        stats = sb("stats", [P, QT, 6])
        mv = sb("mv", [P, QT, 2])
        r_small = sb("r_small", [P, 6, QT])
        xf = sb("xf", [P, QT, D])
        xn = sb("xn", [P, QT, D])
        xnT = sb("xnT", [P, DH, T])
        q_hi = sb("q_hi", [P, DH, T], F32R)
        q_lo = sb("q_lo", [P, DH, T], F32R)
        k_hi = sb("k_hi", [KC, T], F32R)
        k_lo = sb("k_lo", [KC, T], F32R)
        vT = sb("vT", [P, T])
        values = sb("values", [P, 2, QT, KC])
        q_a = sb("q_a", [P, 2, H2, T], F32R)
        q_b = sb("q_b", [P, 2, H2, T], F32R)
        k_a = sb("k_a", [P, 2, T], F32R)
        k_b0 = sb("k_b0", [P, 2, T], F32R)
        k_b1 = sb("k_b1", [P, 2, T], F32R)
        words = {n: t for n, t in (("q_a", q_a[:, :, :, :].bitcast(F32)), ("q_b", q_b[:, :, :, :].bitcast(F32)),
                                   ("k_a", k_a[:, :, :].bitcast(F32)), ("k_b0", k_b0[:, :, :].bitcast(F32)),
                                   ("k_b1", k_b1[:, :, :].bitcast(F32)))}
        row_max = sb("row_max", [P, QT, H2])
        m_hi = sb("m_hi", [H2, T], F32R)
        m_lo = sb("m_lo", [H2, T], F32R)
        probs = sb("probs", [P, 8, T])
        o_pair = sb("o_pair", [P, 2, T])
        sums = sb("sums", [P, T])
        r_sum = sb("r_sum", [P, QT, H2])
        o_tok = sb("o_tok", [P, QT, D])
        oT = sb("oT", [P, DH, T])
        x1_res = sb("x1_res", [P, QT, D])
        xf_res = sb("xf_res", [P, QT, D])
        x2 = sb("x2", [P, QT, D])
        squares = sb("squares", [P, D])
        sq_sum = sb("sq_sum", [P, QT])
        rms2 = sb("rms2", [P, 2, QT])
        xn2 = sb("xn2", [P, QT, D])
        base_sb = sb("base_sb", [P, QT, D])
        moeT = sb("moeT", [P, DH, T])

        ps_s = psum("ps_s", [P, 2, T])
        ps_t = psum("ps_t", [P, 2, T])
        ps_o = psum("ps_o", [P, 2, T])
        ps_r = psum("ps_r", [P, T])
        ps_m = psum("ps_m", [P, T])

        consts = sem("consts")
        set_up = sem("set_up")
        gp_set = sem("gp_set")
        gate_ready = sem("gate_ready")
        x_loaded = sem("x_loaded")
        res_loaded = sem("res_loaded")
        stat_done = sem("stat_done")
        mv_done = sem("mv_done")
        r_step = sem("r_step")
        xf_ready = sem("xf_ready")
        xn_ready = sem("xn_ready")
        xf_stored = sem("xf_stored")
        xT_turned = sem("xT_turned")
        xT_copied = sem("xT_copied")
        kv_done = sem("kv_done")
        k_hi_ready = sem("k_hi_ready")
        k_lo_ready = sem("k_lo_ready")
        vT_ready = sem("vT_ready")
        q_done = sem("q_done")
        q_hi_ready = sem("q_hi_ready")
        q_lo_ready = sem("q_lo_ready")
        v_turned = sem("v_turned")
        v_ready = sem("v_ready")
        slabs_loaded = [[sem(f"slabs_loaded{i}{a}") for a in range(2)] for i in range(2)]
        s_ready = sem("s_ready")
        max_done = sem("max_done")
        m_turned = sem("m_turned")
        m_hi_ready = sem("m_hi_ready")
        m_lo_ready = sem("m_lo_ready")
        m_loaded = sem("m_loaded")
        st_ready = sem("st_ready")
        exp_done = sem("exp_done")
        pv_done = sem("pv_done")
        o_copied = sem("o_copied")
        o_turned = sem("o_turned")
        r_done = sem("r_done")
        o_normed = sem("o_normed")
        oT_turned = sem("oT_turned")
        oT_copied = sem("oT_copied")
        out_done = sem("out_done")
        x2_ready = sem("x2_ready")
        sq_done = sem("sq_done")
        rms_step = sem("rms_step")
        xn2_ready = sem("xn2_ready")
        base_ready = sem("base_ready")
        base_stored = sem("base_stored")
        moe_turned = sem("moe_turned")
        moe_ready = sem("moe_ready")
        moe_stored = sem("moe_stored")

        def rows(ap, b):
            return ap.rearrange("b (t p) d -> b p t d", p=P)[bass.ds(b, 1)].rearrange("o p t d -> p (o t) d")

        SLAB_LOAD = 7 * 16, 3 * 16
        HEAD_ORDER = 0, 2, 1, 3
        MAX_LOAD = 2 * H2 * 16
        TASKS = {(0, 2): ["Y0"], (0, 3): ["Y1"], (1, 0): ["V", "O0"], (1, 1): ["O1"], (1, 2): ["O2"], (1, 3): ["O3"],
                 (2, 0): ["T0"], (2, 1): ["T1"], (2, 2): ["X0"], (2, 3): ["X1"],
                 (3, 0): ["M"], (3, 1): ["W0", "K"], (3, 2): ["W1", "Q0"], (3, 3): ["Q1"]}
        AHEAD = {"X": 2, "K": 2, "Q": 2, "V": 1, "M": 1, "O": -1, "T": -1, "W": -1, "Y": -2}

        SPARE = {("Y", 0): 0, ("Y", 1): 1, ("K", 0): 0, ("Q", 0): 1, ("Q", 1): 0}

        def bank(kind, i):
            return ps_s[:, SPARE[kind, i], :] if (kind, i) in SPARE else ps_m[:, :]

        def tasks(b, place, lo, hi):
            for name in TASKS.get(place, []):
                if lo <= AHEAD[name[0]] <= hi:
                    yield name[0], int(name[1:] or 0), b + AHEAD[name[0]]

        def freed(kind, i, b):
            return {"X": [(xT_copied, 2 * b + i + 1)], "K": [(k_hi_ready, b + 1), (k_lo_ready, b + 1), (vT_ready, b + 1)],
                    "Q": [(q_hi_ready, 2 * b + i + 1), (q_lo_ready, 2 * b + i + 1)], "V": [(v_ready, b + 1)],
                    "M": [(m_hi_ready, b + 1), (m_lo_ready, b + 1)], "O": [(o_normed, QT * b + i + 1)],
                    "T": [(oT_copied, 2 * b + i + 1)], "W": [(x2_ready, 2 * b + i + 1)],
                    "Y": [(moe_ready, 2 * b + i + 1)]}[kind]

        PROLOGUE = [("X", 0, 0), ("X", 1, 0), ("K", 0, 0), ("Q", 0, 0), ("Q", 1, 0), ("V", 0, 0),
                    ("X", 0, 1), ("X", 1, 1), ("K", 0, 1), ("Q", 0, 1), ("Q", 1, 1)]
        EPILOGUE = [("Y", i, B - 2) for i in range(2)] + [("O", i, B - 1) for i in range(QT)] + \
                   [(k, i, B - 1) for k in "TWY" for i in range(2)]

        def all_bodies(eng, body):
            body(0, 0, 0, 2)
            body(1, 1, -1, 2)
            with eng.Fori(2, B - 3, 2) as b:
                body(b, 0, -2, 2)
                body(b + 1, 1, -2, 2)
            body(B - 2, 0, -2, 1)
            body(B - 1, 1, -2, 0)

        block = ctx.enter_context(nc.Block())

        @block.sync
        def _(sp):
            sp.dma_start(ident[:, :], identity).then_inc(consts, 16)
            sp.dma_start(key_init[:, :, :], key_rows).then_inc(consts, 16)
            for dst, src in ((wq_sb, wqT), (wkv_sb, wkvT), (wo_sb, woT)):
                sp.dma_start(dst[:, :, :], src.rearrange("(h p) n -> p h n", p=P)).then_inc(consts, 16)
            sp.dma_start(g1_sb[:, :], g1).then_inc(consts, 16)
            sp.dma_start(g2_sb[:, :], g2).then_inc(consts, 16)
            sp.dma_start(gate[:, :], g_ffn.partition_broadcast(P)).then_inc(consts, 16)

            def load_x(b):
                sp.wait_ge(xn_ready, QT * b)
                sp.wait_ge(xf_ready, QT * b)
                sp.dma_start(xt[:, :, :], rows(x1, b)).then_inc(x_loaded, 16)

            def store_xf(b):
                sp.wait_ge(xf_ready, QT * b + QT)
                sp.dma_start(rows(x_norm, b), xf[:, :, :]).then_inc(xf_stored, 16)

            def load_slabs(b, par, first=False):
                if first and par == 0:
                    sp.wait_ge(set_up, 5)
                if not first:
                    sp.wait_ge(st_ready, 16 * b - 16)
                for s, v in ((k_hi_ready, b + 1), (k_lo_ready, b + 1), (q_hi_ready, 2 * b + 2), (q_lo_ready, 2 * b + 2)):
                    sp.wait_ge(s, v)
                lo, hi = slice(0, KC), slice(KC, P)
                for dst, r, src in (("k_a", lo, k_hi), ("k_a", hi, k_hi), ("k_b0", lo, k_lo), ("k_b1", lo, k_lo)):
                    sp.dma_start(words[dst][r, par, :], src[:, :].bitcast(F32)).then_inc(slabs_loaded[par][0], 16)
                for a in range(2):
                    half = slice(KC * a, KC * a + KC)
                    for dst, r, src in (("q_a", lo, q_hi), ("q_a", hi, q_lo), ("q_b", lo, q_hi)):
                        sp.dma_start(words[dst][r, par, a::2, :], src[half, :, :].bitcast(F32))\
                          .then_inc(slabs_loaded[par][a], 16)

            def load_max(b, par):
                sp.wait_ge(m_hi_ready, b + 1)
                sp.wait_ge(m_lo_ready, b + 1)
                for r, m in ((KC, m_hi), (KC + 1, m_lo)):
                    for h in range(H2):
                        sp.dma_start(words["q_b"][r:r + 1, par, h, :], m[h:h + 1, :].bitcast(F32)).then_inc(m_loaded, 16)

            def load_res(b):
                sp.wait_ge(xf_stored, 16 * b + 16)
                sp.wait_ge(base_ready, b)
                sp.dma_start(x1_res[:, :, :], rows(x1, b)).then_inc(res_loaded, 16)
                sp.dma_start(xf_res[:, :, :], rows(x_norm, b)).then_inc(res_loaded, 16)

            def store_base(b):
                sp.wait_ge(base_ready, b + 1)
                sp.dma_start(rows(base, b), base_sb[:, :, :]).then_inc(base_stored, 16)

            def body(b, par, lo, hi):
                if hi >= 2:
                    load_x(b + 2)
                if hi >= 1 and lo < 0:
                    load_slabs(b + 1, 1 - par)
                if lo < 0:
                    load_res(b - 1)
                if hi >= 2:
                    store_xf(b + 2)
                if lo < 0:
                    store_base(b - 1)
                if hi >= 1:
                    load_max(b + 1, 1 - par)

            load_x(0)
            store_xf(0)
            load_x(1)
            load_slabs(0, 0, True)
            store_xf(1)
            load_slabs(1, 1, True)
            load_max(0, 0)
            all_bodies(sp, body)
            load_res(B - 1)
            store_base(B - 1)
            sp.wait_ge(base_stored, 16 * B)
            sp.wait_ge(moe_stored, 16 * B)

        @block.gpsimd
        def _(pool):
            pool.memset(neg_half[:, :], -0.5).then_inc(gp_set, 1)
            pool.memset(ones[:, :], 1.0).then_inc(gp_set, 1)
            pool.memset(tick[:, :], 0.0).then_inc(gp_set, 1)
            pool.wait_ge(gp_set, 3)
            veps, rstd, square, ms, r2, both = (r_small[:, i, :] for i in range(6))

            def bear_wait(n):
                pool.tensor_tensor(tick[:, n:n + 1], tick[:, 0:1], tick[:, 0:1], ALU.add)

            def normalize(b):
                step = [0]

                def chain(ins):
                    step[0] += 1
                    ins.then_inc(r_step, 1)
                    pool.wait_ge(r_step, 7 * b + step[0])
                    bear_wait(step[0])

                pool.wait_ge(mv_done, QT * b + QT)
                bear_wait(8)
                chain(pool.tensor_scalar(veps, mv[:, :, 1], LN_EPS, None, ALU.add))
                chain(pool.tensor_tensor(rstd, veps, neg_half[:, :], ALU.pow))
                chain(pool.tensor_tensor(square, rstd, rstd, ALU.mult))
                chain(pool.tensor_tensor(ms, square, mv[:, :, 1], ALU.mult))
                chain(pool.tensor_scalar(ms, ms, RMS_EPS, None, ALU.add))
                chain(pool.tensor_tensor(r2, ms, neg_half[:, :], ALU.pow))
                chain(pool.tensor_tensor(both, r2, rstd, ALU.mult))
                pool.wait_ge(xf_stored, 16 * b)
                bear_wait(9)
                for t in range(QT):
                    pool.tensor_scalar(xf[:, t, :], xt[:, t, :], mv[:, t, 0:1], r_small[:, 1, t:t + 1],
                                       ALU.subtract, ALU.mult).then_inc(xf_ready, 1)

            def rms(b):
                pool.wait_ge(sq_done, QT * b + QT)
                bear_wait(10)
                pool.tensor_scalar(rms2[:, 0, :], sq_sum[:, :], 1.0 / D, RMS_EPS, ALU.mult, ALU.add).then_inc(rms_step, 1)
                pool.wait_ge(rms_step, 2 * b + 1)
                pool.tensor_tensor(rms2[:, 1, :], rms2[:, 0, :], neg_half[:, :], ALU.pow).then_inc(rms_step, 1)

            def body(b, par, lo, hi):
                if hi >= 2:
                    normalize(b + 2)
                if lo < 0:
                    rms(b - 1)

            normalize(0)
            normalize(1)
            all_bodies(pool, body)
            rms(B - 1)

        @block.scalar
        def _(act):
            act.wait_ge(consts, 16 * 8)
            act.activation(gate[:, :], gate[:, :], ACT.Tanh).then_inc(gate_ready, 1)

            def task(kind, i, b, par=0, first=False):
                ps = bank(kind, i)
                if kind == "X":
                    act.wait_ge(xT_turned, 2 * b + i + 1)
                    act.mul(xnT[:, i, :], ps[:, :], g1_sb[:, i:i + 1]).then_inc(xT_copied, 1)
                elif kind == "K":
                    act.wait_ge(kv_done, b + 1)
                    if not first:
                        for a in range(2):
                            act.wait_ge(slabs_loaded[1 - par][a], SLAB_LOAD[a] * ((b - 1) // 2 + 1))
                    act.wait_ge(v_turned, b)
                    act.copy(vT[:, :], ps[:, :]).then_inc(vT_ready, 1)
                    act.copy(k_hi[:, :], ps[0:KC, :]).then_inc(k_hi_ready, 1)
                elif kind == "Q":
                    act.wait_ge(q_done, 2 * b + i + 1)
                    act.copy(q_hi[:, i, :], ps[:, :]).then_inc(q_hi_ready, 1)
                elif kind == "V":
                    act.wait_ge(v_turned, b + 1)
                    act.wait_ge(pv_done, QT * b - QT if not first else 0)
                    act.copy(values[:, par, :, :], ps[:, :].rearrange("p (t d) -> p t d", d=2 * KC)[:, :, KC:])\
                       .then_inc(v_ready, 1)
                elif kind == "M":
                    act.wait_ge(m_turned, b + 1)
                    act.wait_ge(m_loaded, MAX_LOAD * b)
                    act.mul(m_hi[:, :], ps[0:H2, :], -1.0).then_inc(m_hi_ready, 1)
                elif kind == "T":
                    act.wait_ge(oT_turned, 2 * b + i + 1)
                    act.copy(oT[:, i, :], ps[:, :]).then_inc(oT_copied, 1)
                elif kind == "W":
                    act.wait_ge(x2_ready, 2 * b + i + 1)
                    for t in range(2 * i, 2 * i + 2):
                        if t > 0:
                            act.wait_ge(sq_done, QT * b + t)
                        act.activation(squares[:, :], x2[:, t, :], ACT.Square, accum_out=sq_sum[:, t:t + 1]).then_inc(sq_done, 1)
                elif kind == "Y":
                    act.wait_ge(moe_turned, 2 * b + i + 1)
                    act.wait_ge(moe_stored, 16 * b)
                    act.mul(moeT[:, i, :], ps[:, :], g2_sb[:, i:i + 1]).then_inc(moe_ready, 1)
                    if i == 1:
                        act.wait_ge(moe_ready, 2 * b + 2)
                        act.dma_start(x_moe[bass.ds(b, 1)].rearrange("o p h t -> p (o h) t"), moeT[:, :, :])\
                           .then_inc(moe_stored, 16)

            def copy_o(b, first=False):
                act.wait_ge(pv_done, QT * b + QT)
                if not first:
                    act.wait_ge(o_turned, QT * b)
                for i in range(2):
                    act.copy(o_pair[:, i, :], ps_o[:, i, :]).then_inc(o_copied, 1)
                act.copy(sums[:, :], ps_r[:, :]).then_inc(o_copied, 1)

            def par_of(kind, par):
                return (par + AHEAD[kind]) % 2

            def body(b, par, lo, hi):
                for k in range(4):
                    for j in range(H2):
                        i = 4 * k + j
                        act.wait_ge(st_ready, 16 * b + i + 1)
                        if lo < 0 or i >= 8:
                            act.wait_ge(pv_done, QT * b + k - 1)
                        act.activation(probs[:, i % 8, :], ps_t[:, i % 2, :], ACT.Exp, scale=KC ** -0.5).then_inc(exp_done, 1)
                        if (k, j) == (0, 3) and lo < 0:
                            copy_o(b - 1)
                        for kind, n, bb in tasks(b, (k, j), lo, hi):
                            task(kind, n, bb, par_of(kind, par))

            for kind, i, b in PROLOGUE:
                task(kind, i, b, b % 2, b == 0)
            task("M", 0, 0)
            all_bodies(act, body)
            copy_o(B - 1)
            for kind, i, b in EPILOGUE:
                task(kind, i, b)

        @block.vector
        def _(dve):
            dve.wait_ge(consts, 16 * 8)
            zeros = key_init[:, 0:1, :]
            for k in (0, 1):
                q = (q_a, q_b)[k]
                dve.tensor_scalar(q[:, :, :, :].rearrange("p a h t -> p (a h) t"), zeros.broadcast_to([P, 2 * H2, T]),
                                  0.0, None, ALU.mult).then_inc(set_up, 1)
            dve.tensor_scalar(k_a[:, :, :], zeros.broadcast_to([P, 2, T]), 0.0, None, ALU.mult).then_inc(set_up, 1)
            dve.tensor_scalar(k_b0[:, :, :], zeros.broadcast_to([P, 2, T]), 0.0, None, ALU.mult).then_inc(set_up, 1)
            dve.tensor_copy(k_b1[:, :, :], key_init[:, 1:2, :].broadcast_to([P, 2, T])).then_inc(set_up, 1)
            dve.wait_ge(gate_ready, 1)

            def statistics(b):
                dve.wait_ge(x_loaded, 16 * b + 16)
                for t in range(QT):
                    dve.bn_stats(stats[:, t, :], xt[:, t, :]).then_inc(stat_done, 1)
                dve.wait_ge(stat_done, QT * b + QT)
                dve.tensor_copy(veps_tick[:, 0:1], stats[:, 0, 0:1])
                for t in range(QT):
                    dve.bn_aggr(mv[:, t, :], stats[:, t, :]).then_inc(mv_done, 1)

            def normalize(b):
                dve.wait_ge(r_step, 7 * b + 7)
                dve.wait_ge(xT_turned, 2 * b)
                for t in range(QT):
                    dve.tensor_scalar(xn[:, t, :], xt[:, t, :], mv[:, t, 0:1], r_small[:, 5, t:t + 1],
                                      ALU.subtract, ALU.mult).then_inc(xn_ready, 1)

            def normalize_moe(b):
                dve.wait_ge(rms_step, 2 * b + 2)
                dve.wait_ge(moe_turned, 2 * b)
                for t in range(QT):
                    dve.tensor_scalar(xn2[:, t, :], x2[:, t, :], rms2[:, 1, t:t + 1], None, ALU.mult).then_inc(xn2_ready, 1)

            def task(kind, i, b):
                ps = bank(kind, i)
                if kind == "K":
                    dve.wait_ge(k_hi_ready, b + 1)
                    dve.tensor_tensor(k_lo[:, :], ps[0:KC, :], k_hi[:, :].bitcast(F32), ALU.subtract).then_inc(k_lo_ready, 1)
                elif kind == "Q":
                    dve.wait_ge(q_hi_ready, 2 * b + i + 1)
                    dve.tensor_tensor(q_lo[:, i, :], ps[:, :], q_hi[:, i, :].bitcast(F32), ALU.subtract).then_inc(q_lo_ready, 1)
                elif kind == "M":
                    dve.wait_ge(m_hi_ready, b + 1)
                    dve.scalar_tensor_tensor(out=m_lo[:, :], in0=ps[0:H2, :], scalar=-1.0, in1=m_hi[:, :].bitcast(F32),
                                             op0=ALU.mult, op1=ALU.subtract).then_inc(m_lo_ready, 1)
                elif kind == "O":
                    dve.wait_ge(o_turned, QT * b + i + 1)
                    dve.reciprocal(r_sum[:, i, :], ps[:, 2 * P:3 * P].rearrange("p (h e) -> p h e", e=32)[:, :, 0])\
                       .then_inc(r_done, 1)
                    dve.wait_ge(r_done, QT * b + i + 1)
                    dve.tensor_tensor(o_tok[:, i, :].rearrange("p (h d) -> p h d", d=KC),
                                      ps[:, 0:2 * P].rearrange("p (h d) -> p h d", d=KC),
                                      r_sum[:, i, :].unsqueeze(2).broadcast_to([P, H2, KC]), ALU.mult).then_inc(o_normed, 1)
                elif kind == "W":
                    s = slice(2 * i, 2 * i + 2)
                    dve.wait_ge(out_done, 2 * b + i + 1)
                    dve.wait_ge(res_loaded, 32 * b + 32)
                    dve.wait_ge(xn2_ready, QT * b)
                    dve.tensor_tensor(x2[:, s, :].rearrange("p t d -> p (t d)"), ps[:, :],
                                      xf_res[:, s, :].rearrange("p t d -> p (t d)"), ALU.add).then_inc(x2_ready, 1)
                    if i == 1:
                        dve.wait_ge(x2_ready, 2 * b + 2)
                        dve.wait_ge(base_stored, 16 * b)
                        dve.scalar_tensor_tensor(out=base_sb[:, :, :].rearrange("p t d -> p (t d)"),
                                                 in0=x2[:, :, :].rearrange("p t d -> p (t d)"), scalar=gate[:, 0:1],
                                                 in1=x1_res[:, :, :].rearrange("p t d -> p (t d)"),
                                                 op0=ALU.mult, op1=ALU.add).then_inc(base_ready, 1)

            def row_maximum(b, n, t):
                i, h = 4 * n + t, HEAD_ORDER[n]
                dve.wait_ge(s_ready, 16 * b + i + 1)
                if i == 0:
                    dve.wait_ge(m_turned, b)
                dve.tensor_reduce(row_max[:, t, h:h + 1], ps_s[:, i % 2, :], AX.X, ALU.max).then_inc(max_done, 1)

            def body(b, par, lo, hi):
                for k in range(4):
                    for j in range(H2):
                        if (k, j) == (0, 1) and lo <= -2:
                            normalize_moe(b - 2)
                        if (k, j) == (0, 2) and hi >= 2:
                            statistics(b + 2)
                        if (k, j) == (1, 3) and hi >= 2:
                            normalize(b + 2)
                        if k in (1, 2) and hi >= 1:
                            for t in range(2):
                                row_maximum(b + 1, 2 * k - 2 + j // 2, 2 * (j % 2) + t)
                        for t in tasks(b, (k, j), lo, hi):
                            task(*t)

            statistics(0)
            normalize(0)
            for n, (kind, i, b) in enumerate(PROLOGUE):
                if n == 5:
                    statistics(1)
                    normalize(1)
                task(kind, i, b)
            for h in range(H2):
                for t in range(QT):
                    row_maximum(0, h, t)
            task("M", 0, 0)
            all_bodies(dve, body)
            normalize_moe(B - 2)
            for t in EPILOGUE:
                if t == ("Y", 0, B - 1):
                    normalize_moe(B - 1)
                task(*t)

        @block.tensor
        def _(pe):
            pe.wait_ge(consts, 16 * 8)
            last_task = {0: None, 1: None, None: None}

            def task(kind, i, b):
                ps = bank(kind, i)
                if kind == "X":
                    if i == 0:
                        pe.wait_ge(xn_ready, QT * b + QT)
                    for t in range(QT):
                        mm = pe.transpose(ps[:, t * P:(t + 1) * P], xn[:, t, i * P:(i + 1) * P], ident[:, :])
                    mm.then_inc(xT_turned, 1)
                elif kind == "K":
                    pe.wait_ge(xT_copied, 2 * b + 2)
                    for h in range(DH):
                        mm = pe.matmul(ps[:, :], wkv_sb[:, h, :], xnT[:, h, :], start=(h == 0), stop=(h == DH - 1))
                    mm.then_inc(kv_done, 1)
                elif kind == "Q":
                    for h in range(DH):
                        mm = pe.matmul(ps[:, :], wq_sb[:, h, i * P:(i + 1) * P], xnT[:, h, :],
                                       start=(h == 0), stop=(h == DH - 1))
                    mm.then_inc(q_done, 1)
                elif kind == "V":
                    pe.wait_ge(vT_ready, b + 1)
                    for t in range(QT):
                        mm = pe.transpose(ps[:, t * P:(t + 1) * P], vT[:, t * P:(t + 1) * P], ident[:, :])
                    mm.then_inc(v_turned, 1)
                elif kind == "M":
                    pe.wait_ge(max_done, 16 * b + 16)
                    for t in range(QT):
                        mm = pe.transpose(ps[0:H2, t * P:(t + 1) * P], row_max[:, t, :], ident[:, :])
                    mm.then_inc(m_turned, 1)
                elif kind == "O":
                    pe.wait_ge(o_copied, 3 * b + 3)
                    for n, src in enumerate((o_pair[:, 0, :], o_pair[:, 1, :], sums[:, :])):
                        mm = pe.transpose(ps[:, n * P:(n + 1) * P], src[:, i * P:(i + 1) * P], ident[:, :])
                    mm.then_inc(o_turned, 1)
                elif kind == "T":
                    if i == 0:
                        pe.wait_ge(o_normed, QT * b + QT)
                    for t in range(QT):
                        mm = pe.transpose(ps[:, t * P:(t + 1) * P], o_tok[:, t, i * P:(i + 1) * P], ident[:, :])
                    mm.then_inc(oT_turned, 1)
                elif kind == "W":
                    if i == 0:
                        pe.wait_ge(oT_copied, 2 * b + 2)
                    for t in range(2 * i, 2 * i + 2):
                        for h in range(DH):
                            mm = pe.matmul(ps[:, (t % 2) * D:(t % 2 + 1) * D], oT[:, h, t * P:(t + 1) * P],
                                           wo_sb[:, h, :], start=(h == 0), stop=(h == DH - 1))
                    mm.then_inc(out_done, 1)
                elif kind == "Y":
                    pe.wait_ge(xn2_ready, QT * b + QT)
                    for t in range(QT):
                        mm = pe.transpose(ps[:, t * P:(t + 1) * P], xn2[:, t, i * P:(i + 1) * P], ident[:, :])
                    mm.then_inc(moe_turned, 1)

            def max_scores(b, par, n, t):
                i = 4 * n + t
                if t == 0 and n % 2 == 0:
                    pe.wait_ge(slabs_loaded[par][n // 2], SLAB_LOAD[n // 2] * (b // 2 + 1))
                if i < 2 and last_task[i] is not None:
                    wait_freed(i, b, 1)
                if i >= 2:
                    pe.wait_ge(max_done, 16 * b + i - 1)
                h = HEAD_ORDER[n]
                q = slice(t * P, (t + 1) * P)
                pe.matmul(ps_s[:, i % 2, :], q_a[:, par, h, q], k_a[:, par, :], start=True, stop=False)
                pe.matmul(ps_s[:, i % 2, :], q_b[:, par, h, q], k_b0[:, par, :], start=False, stop=True).then_inc(s_ready, 1)

            def exp_scores(b, par, c, h, first):
                i = 4 * c + h
                if i == 0:
                    pe.wait_ge(m_loaded, MAX_LOAD * (b + 1))
                if not (first and i < 2):
                    pe.wait_ge(exp_done, 16 * b + i - 1)
                k = slice(c * P, (c + 1) * P)
                pe.matmul(ps_t[:, i % 2, :], k_a[:, par, k], q_a[:, par, h, :], start=True, stop=False)
                pe.matmul(ps_t[:, i % 2, :], k_b1[:, par, k], q_b[:, par, h, :], start=False, stop=True).then_inc(st_ready, 1)

            def weigh_values(b, par, c, pair, first):
                pe.wait_ge(exp_done, 16 * b + 4 * c + 2 * pair + 2)
                if c == 0 and pair == 0:
                    pe.wait_ge(v_ready, b + 1)
                    if not first:
                        pe.wait_ge(o_copied, 3 * b)
                for a in range(2):
                    pe.matmul(ps_o[KC * a:KC * a + KC, pair, :], values[:, par, c, :], probs[:, (4 * c + 2 * pair + a) % 8, :],
                              start=(c == 0), stop=(c == QT - 1), skip_group_check=True)

            def sum_probs(b, c):
                for h in range(H2):
                    mm = pe.matmul(ps_r[32 * h:32 * h + 32, :], ones[:, :], probs[:, (4 * c + h) % 8, :],
                                   start=(c == 0), stop=(c == QT - 1), skip_group_check=True)
                mm.then_inc(pv_done, 1)

            def body(b, par, lo, hi):
                first = lo == 0
                for k in range(4):
                    for j in range(H2):
                        if k in (1, 2) and hi >= 1:
                            for t in range(2):
                                max_scores(b + 1, 1 - par, 2 * k - 2 + j // 2, 2 * (j % 2) + t)
                        exp_scores(b, par, k, j, first)
                        if j % 2 == 1 and (k > 0 or not first):
                            bb, pp, c = (b, par, k - 1) if k else (b - 1, 1 - par, 3)
                            weigh_values(bb, pp, c, j // 2, first and k == 1)
                            if j == 3:
                                sum_probs(bb, c)
                        for kind, n, bb in tasks(b, (k, j), lo, hi):
                            run(kind, n, bb, AHEAD[kind])

            def wait_freed(place, b, ahead):
                pk, pn, pahead = last_task[place]
                for s, v in freed(pk, pn, b + (pahead - ahead)):
                    pe.wait_ge(s, v)

            def run(kind, n, b, ahead):
                place = SPARE.get((kind, n))
                if last_task[place] is not None:
                    wait_freed(place, b, ahead)
                if place is not None and (kind, n) != ("Q", 1) and scored[0]:
                    pe.wait_ge(max_done, 16 * (b - ahead + 1) + 16 * (kind in "KQ"))
                task(kind, n, b)
                last_task[place] = (kind, n, ahead)

            scored = [False]
            for kind, i, b in PROLOGUE:
                run(kind, i, b, b)
            for place in (0, 1):
                last_task[place] = last_task[place][:2] + (last_task[place][2] + 1,)
            for h in range(H2):
                for t in range(QT):
                    max_scores(0, 0, h, t)
            scored[0] = True
            run("M", 0, 0, 0)
            for place in (0, 1):
                last_task[place] = None
            body(0, 0, 0, 2)
            def bodies():
                def nxt():
                    for place, t in last_task.items():
                        last_task[place] = (t[0], t[1], t[2] - 1)
                nxt()
                body(1, 1, -1, 2)
                nxt()
                with pe.Fori(2, B - 3, 2) as b:
                    body(b, 0, -2, 2)
                    nxt()
                    body(b + 1, 1, -2, 2)
                    nxt()
                body(B - 2, 0, -2, 1)
                nxt()
                body(B - 1, 1, -2, 0)

            bodies()
            for pair in range(2):
                weigh_values(B - 1, 1, QT - 1, pair, False)
            sum_probs(B - 1, QT - 1)
            for place, t in last_task.items():
                last_task[place] = (t[0], t[1], B - 1 + t[2])
            scored[0] = False
            for kind, i, b in EPILOGUE:
                run(kind, i, b, b)


E = 8
F = 256
N_W = E + 1


def experts(nc, x_moe, base, g_ffn, wrT, bias, w13T, w2T, iota, identity, out):
    with ExitStack() as ctx:
        def sb(name, shape, dt=F32):
            return ctx.enter_context(nc.sbuf_tensor("mo_" + name, shape, dt))

        def psum(name, shape):
            return ctx.enter_context(nc.psum_tensor("mo_" + name, shape, F32))

        def sem(name):
            return ctx.enter_context(nc.semaphore("mo_" + name))

        wr_sb = sb("wr", [P, DH, E])
        bias_sb = sb("bias", [P, E])
        gate = sb("gate", [P, 1])
        tick = sb("tick", [P, 1])
        iota_sb = sb("iota", [P, E])
        stage = sb("stage", [P, 2, 3, DH * F])
        w_hi = sb("w_hi", [P, N_W, 3, DH, F], F32R)
        w_lo = sb("w_lo", [P, N_W, 3, DH, F], F32R)
        xT = sb("xT", [P, DH, T])
        x_hi = sb("x_hi", [P, DH, T], F32R)
        x_lo = sb("x_lo", [P, DH, T], F32R)
        logits = sb("logits", [P, QT, E])
        top = sb("top", [P, 1, QT])
        probs = sb("probs", [P, QT, E])
        psums = sb("psums", [P, QT])
        best = sb("best", [P, QT, E])
        where = sb("where", [P, QT, E], U32)
        where_f = sb("where_f", [P, QT, 2])
        w_top = sb("w_top", [P, 4, QT])
        coef = sb("coef", [P, QT, N_W])
        picked = sb("picked", [P, 2, E])
        s_act = sb("s_act", [P, 2, T])
        h_full = sb("h_full", [P, 2, T])
        h_hi = sb("h_hi", [P, 2, 2, T], F32R)
        h_lo = sb("h_lo", [P, 2, 2, T], F32R)
        acc = sb("acc", [P, 2, QT, D])

        ps_h = psum("ps_h", [P, 2, 2, T])
        ps_y = psum("ps_y", [P, 2, 2, D])
        ps_r = psum("ps_r", [P, T])

        consts = sem("consts")
        gate_ready = sem("gate_ready")
        w_loaded = [sem(f"w_loaded{i}") for i in range(2)]
        hi_ready = sem("w_hi_ready")
        lo_ready = sem("w_lo_ready")
        x_loaded = sem("x_loaded")
        base_loaded = sem("base_loaded")
        xh_ready = sem("xh_ready")
        xl_ready = sem("xl_ready")
        logit_done = sem("logit_done")
        route = sem("route")
        exp_done = sem("exp_done")
        coef_ready = sem("coef_ready")
        h_done = sem("h_done")
        silu_done = sem("silu_done")
        h_ready = sem("h_ready")
        hh_ready = sem("hh_ready")
        hl_ready = sem("hl_ready")
        y_done = sem("y_done")
        acc_step = sem("acc_step")
        stored = sem("stored")

        def rows(ap, b):
            return ap.rearrange("b (t p) d -> b p t d", p=P)[bass.ds(b, 1)].rearrange("o p t d -> p (o t) d")

        U = 2 * N_W
        block = ctx.enter_context(nc.Block())

        @block.sync
        def _(sp):
            sp.dma_start(wr_sb[:, :, :], wrT.rearrange("(h p) n -> p h n", p=P)).then_inc(consts, 16)
            sp.dma_start(bias_sb[:, :], bias.partition_broadcast(P)).then_inc(consts, 16)
            sp.dma_start(gate[:, :], g_ffn.partition_broadcast(P)).then_inc(consts, 16)
            sp.dma_start(iota_sb[:, :], iota.partition_broadcast(P)).then_inc(consts, 16)

            def load(b):
                sp.wait_ge(xh_ready, b)
                sp.wait_ge(xl_ready, b)
                sp.wait_ge(logit_done, b)
                sp.dma_start(xT[:, :, :], x_moe[bass.ds(b, 1)].rearrange("o p h t -> p (o h) t")).then_inc(x_loaded, 16)

            def load_w(e):
                if e >= 2:
                    sp.wait_ge(hi_ready, e - 1)
                    sp.wait_ge(lo_ready, e - 1)
                for i, w in enumerate((w13T[e][:, 0:F], w13T[e][:, F:2 * F], w2T[e])):
                    sp.dma_start(stage[:, e % 2, i, :].rearrange("p (h f) -> p h f", f=F),
                                 w.rearrange("(h p) f -> p h f", p=P)).then_inc(w_loaded[e % 2], 16)

            load(0)
            for e in range(N_W):
                load_w(e)
            sp.dma_start(acc[:, 0, :, :], rows(base, 0)).then_inc(base_loaded, 16)

            with sp.Fori(0, B - 1) as b:
                load(b + 1)
                sp.wait_ge(acc_step, (b + 1) * 4 * N_W)
                sp.dma_start(rows(out, b), acc[:, 0, :, :]).then_inc(stored, 16)
                sp.wait_ge(stored, b * 16 + 16)
                sp.dma_start(acc[:, 0, :, :], rows(base, b + 1)).then_inc(base_loaded, 16)
            sp.wait_ge(acc_step, B * 4 * N_W)
            sp.dma_start(rows(out, B - 1), acc[:, 0, :, :]).then_inc(stored, 16)
            sp.wait_ge(stored, 16 * B)

        @block.scalar
        def _(act):
            act.wait_ge(consts, 16 * 4)
            act.activation(gate[:, :], gate[:, :], ACT.Tanh).then_inc(gate_ready, 1)
            for e in range(N_W):
                act.wait_ge(w_loaded[e % 2], 48 * (e // 2 + 1))
                act.copy(w_hi[:, e, :, :, :].rearrange("p i h f -> p (i h f)"), stage[:, e % 2, :, :].rearrange("p i f -> p (i f)"))\
                   .then_inc(hi_ready, 1)

            def body(b):
                act.wait_ge(x_loaded, 16 * b + 16)
                act.wait_ge(h_done, U * b)
                act.copy(x_hi[:, :, :], xT[:, :, :]).then_inc(xh_ready, 1)
                act.wait_ge(route, 11 * b + 3)
                act.activation(probs[:, :, :], logits[:, :, :], ACT.Exp).then_inc(exp_done, 1)
                act.wait_ge(route, 11 * b + 8)
                act.activation(w_top[:, 1, :], w_top[:, 0, :], ACT.Exp).then_inc(exp_done, 1)
                for u in range(U):
                    act.wait_ge(h_done, U * b + u + 1)
                    act.wait_ge(h_ready, U * b + u - 1 if u >= 1 else U * b)
                    act.activation(s_act[:, u % 2, :], ps_h[:, u % 2, 0, :], ACT.Silu).then_inc(silu_done, 1)
                    act.wait_ge(h_ready, U * b + u + 1)
                    if u >= 4:
                        act.wait_ge(y_done, 2 * N_W * b + 2 * (u // 2 - 1))
                    act.copy(h_hi[:, (u // 2) % 2, u % 2, :], h_full[:, u % 2, :]).then_inc(hh_ready, 1)

            with act.Fori(0, B) as b:
                body(b)

        @block.vector
        def _(dve):
            dve.wait_ge(consts, 16 * 4)
            dve.wait_ge(gate_ready, 1)
            for e in range(N_W):
                dve.wait_ge(hi_ready, e + 1)
                dve.tensor_tensor(w_lo[:, e, :, :, :].rearrange("p i h f -> p (i h f)"), stage[:, e % 2, :, :].rearrange("p i f -> p (i f)"),
                                  w_hi[:, e, :, :, :].rearrange("p i h f -> p (i h f)").bitcast(F32), ALU.subtract).then_inc(lo_ready, 1)

            def body(b):
                step = [0]

                def chain(ins):
                    step[0] += 1
                    ins.then_inc(route, 1)
                    dve.wait_ge(route, 11 * b + step[0])
                    dve.tensor_copy(tick[:, :], gate[:, :])

                dve.wait_ge(xh_ready, b + 1)
                dve.tensor_tensor(x_lo[:, :, :], xT[:, :, :], x_hi[:, :, :].bitcast(F32), ALU.subtract).then_inc(xl_ready, 1)
                dve.wait_ge(logit_done, b + 1)
                L = ps_r[:, 0:QT * E].rearrange("p (t e) -> p t e", e=E)
                chain(dve.tensor_tensor(logits[:, :, :], L, bias_sb[:, :].unsqueeze(1).broadcast_to([P, QT, E]), ALU.add))
                chain(dve.tensor_reduce(top[:, 0, :], logits[:, :, :], AX.X, ALU.max))
                chain(dve.tensor_tensor(logits[:, :, :], logits[:, :, :], top[:, 0, :].unsqueeze(2).broadcast_to([P, QT, E]), ALU.subtract))
                dve.wait_ge(exp_done, 2 * b + 1)
                chain(dve.tensor_reduce(psums[:, :], probs[:, :, :], AX.X, ALU.add))
                chain(dve.reciprocal(psums[:, :], psums[:, :]))
                chain(dve.tensor_tensor(probs[:, :, :], probs[:, :, :], psums[:, :].unsqueeze(2).broadcast_to([P, QT, E]), ALU.mult))
                for t in range(QT):
                    ins = dve.max(best[:, t, :], probs[:, t, :])
                chain(ins)
                chain(dve.tensor_tensor(w_top[:, 0, :], best[:, :, 1], best[:, :, 0], ALU.subtract))
                for t in range(QT):
                    ins = dve.max_index(where[:, t, :], best[:, t, :], probs[:, t, :])
                chain(ins)
                chain(dve.tensor_copy(where_f[:, :, :], where[:, :, 0:2]))
                dve.wait_ge(exp_done, 2 * b + 2)
                chain(dve.tensor_scalar(w_top[:, 2, :], w_top[:, 1, :], 1.0, None, ALU.add))
                n = [0]

                def link(ins):
                    n[0] += 1
                    ins.then_inc(coef_ready, 1)
                    dve.wait_ge(coef_ready, 15 * b + n[0])

                link(dve.reciprocal(w_top[:, 2, :], w_top[:, 2, :]))
                link(dve.tensor_scalar(w_top[:, 2, :], w_top[:, 2, :], gate[:, 0:1], None, ALU.mult))
                dve.tensor_copy(coef[:, :, 0], gate[:, 0:1].broadcast_to([P, QT]))
                link(dve.tensor_tensor(w_top[:, 3, :], w_top[:, 1, :], w_top[:, 2, :], ALU.mult))
                for t in range(QT):
                    for j in range(2):
                        ins = dve.tensor_scalar(picked[:, j, :], iota_sb[:, :], where_f[:, t, j:j + 1], w_top[:, 2 + j, t:t + 1],
                                                ALU.is_equal, ALU.mult)
                        link(ins)
                    link(dve.tensor_tensor(coef[:, t, 1:N_W], picked[:, 0, :], picked[:, 1, :], ALU.add))

                dve.wait_ge(base_loaded, 16 * b + 16)
                for u in range(U + 1):
                    if u < U:
                        dve.wait_ge(silu_done, U * b + u + 1)
                        dve.wait_ge(hl_ready, U * b + u - 1 if u >= 1 else U * b)
                        dve.wait_ge(hh_ready, U * b + u - 1 if u >= 1 else U * b)
                        dve.tensor_tensor(h_full[:, u % 2, :], s_act[:, u % 2, :], ps_h[:, u % 2, 1, :], ALU.mult).then_inc(h_ready, 1)
                        dve.wait_ge(hh_ready, U * b + u + 1)
                        dve.tensor_tensor(h_lo[:, (u // 2) % 2, u % 2, :], h_full[:, u % 2, :],
                                          h_hi[:, (u // 2) % 2, u % 2, :].bitcast(F32), ALU.subtract).then_inc(hl_ready, 1)
                    if u >= 2 and u % 2 == 0:
                        e = u // 2 - 1
                        for t in range(QT):
                            dve.wait_ge(y_done, 2 * (N_W * b + e) + t // 2 + 1)
                            dve.wait_ge(acc_step, QT * (N_W * b + e))
                            dve.scalar_tensor_tensor(out=acc[:, 0, t, :], in0=ps_y[:, t // 2, t % 2, :], scalar=coef[:, t, e:e + 1],
                                                     in1=acc[:, 0, t, :], op0=ALU.mult, op1=ALU.add).then_inc(acc_step, 1)

            with dve.Fori(0, B) as b:
                body(b)

        @block.tensor
        def _(pe):
            pe.wait_ge(consts, 16 * 4)

            def body(b):
                pe.wait_ge(x_loaded, 16 * b + 16)
                pe.wait_ge(coef_ready, 15 * b)
                for t in range(QT):
                    for h in range(DH):
                        mm = pe.matmul(ps_r[:, t * E:(t + 1) * E], xT[:, h, t * P:(t + 1) * P], wr_sb[:, h, :],
                                       start=(h == 0), stop=(h == DH - 1))
                mm.then_inc(logit_done, 1)
                pe.wait_ge(xl_ready, b + 1)
                for u in range(U + 2):
                    if u < U:
                        e, f = u // 2, u % 2
                        pe.wait_ge(lo_ready, e + 1)
                        pe.wait_ge(h_ready, U * b + u - 1 if u >= 1 else U * b)
                        for g in range(2):
                            n = 0
                            for h in range(DH):
                                for w, x in ((w_hi, x_hi), (w_hi, x_lo), (w_lo, x_hi)):
                                    mm = pe.matmul(ps_h[:, u % 2, g, :], w[:, e, g, h, f * P:(f + 1) * P], x[:, h, :],
                                                   start=(n == 0), stop=(n == 5))
                                    n += 1
                        mm.then_inc(h_done, 1)
                    if u >= 2 and u % 2 == 1:
                        e = u // 2 - 1
                        pe.wait_ge(hl_ready, U * b + 2 * e + 2)
                        for t2 in range(2):
                            pe.wait_ge(acc_step, QT * (N_W * b + e - 1) + 2 * t2 + 2 if e >= 1 else QT * N_W * b)
                            for t in range(2):
                                n = 0
                                for h in range(2):
                                    for hh, w in ((h_hi, w_hi), (h_hi, w_lo), (h_lo, w_hi)):
                                        tt = 2 * t2 + t
                                        mm = pe.matmul(ps_y[:, t2, t, :], hh[:, e % 2, h, tt * P:(tt + 1) * P], w[:, e, 2, h, :],
                                                       start=(n == 0), stop=(n == 5))
                                        n += 1
                            mm.then_inc(y_done, 1)

            with pe.Fori(0, B) as b:
                body(b)


def program(nc, ins, out):
    x1 = nc.dram_tensor("x1_scratch", [B, T, D], F32).ap()
    x_norm = nc.dram_tensor("x_norm_scratch", [B, T, D], F32).ap()
    base = nc.dram_tensor("base_scratch", [B, T, D], F32).ap()
    x_moe = nc.dram_tensor("x_moe_scratch", [B, P, DH, T], F32).ap()
    cross_attention(nc, ins["x"], ins["ctxT"], ins["g_xattn"], ins["wq"], ins["bq"], ins["wk"], ins["bk"],
                    ins["wv"], ins["bv"], ins["wo"], ins["bo"], ins["identity"], ins["key_rows"], x1)
    self_attention(nc, x1, ins["g_ffn"], ins["g1"], ins["wqT"], ins["wkvT"], ins["woT"], ins["g2"],
                   ins["identity"], ins["key_rows2"], x_norm, base, x_moe)
    experts(nc, x_moe, base, ins["g_ffn"], ins["wrT"], ins["expert_bias"], ins["w13T"], ins["w2T"],
            ins["iota"], ins["identity"], out)


def kernel(**inputs):
    import numpy as np
    import concourse.bacc as bacc
    from concourse.bass_utils import run_bass_kernel_spmd

    xa = {k[len("L0_xattn_"):]: np.asarray(v) for k, v in inputs.items() if k.startswith("L0_xattn_")}
    ff = {k[len("L0_ffn_"):]: np.asarray(v) for k, v in inputs.items() if k.startswith("L0_ffn_")}

    def slab_order(w):
        return w.reshape(-1, PACKS, 2, 2, DK).transpose(0, 2, 1, 3, 4).reshape(-1, D)

    def columns(v):
        return v.reshape(DH, P).T

    key_rows = np.zeros((P, 2, T), np.float32)
    for place in range(2):
        key_rows[96 + place, place] = 1
        key_rows[98 + place, place] = 1
    key_rows2 = np.zeros((P, 2, T), np.float32)
    key_rows2[KC:KC + 2, 1] = 1

    arrays = {
        "x": inputs["x"], "ctxT": np.asarray(inputs["ctx_512"]).transpose(0, 2, 1), "g_xattn": inputs["g_xattn"],
        "wq": slab_order(xa["Wq"]), "bq": columns(slab_order(xa["bq"]).reshape(D)),
        "wk": slab_order(xa["Wk"]), "bk": columns(slab_order(xa["bk"]).reshape(D)),
        "wv": xa["Wv"], "bv": xa["bv"], "wo": xa["Wo"], "bo": xa["bo"],
        "g_ffn": inputs["g_ffn"], "g1": columns(ff["g1"]), "g2": columns(ff["g2"]), "wqT": ff["Wq"].T,
        "wkvT": np.concatenate([ff["Wkc"].T, ff["Wvc"].T], 1), "woT": ff["Wo"].T,
        "wrT": ff["Wr"].T, "expert_bias": ff["expert_bias"],
        "w13T": np.concatenate([np.concatenate([ff["sW1"][None], ff["eW1"]]).transpose(0, 2, 1),
                                np.concatenate([ff["sW3"][None], ff["eW3"]]).transpose(0, 2, 1)], 2),
        "w2T": np.concatenate([ff["sW2"][None], ff["eW2"]]).transpose(0, 2, 1),
        "identity": np.eye(P, dtype=np.float32), "key_rows": key_rows, "key_rows2": key_rows2,
        "iota": np.arange(E, dtype=np.float32),
    }
    nc = bacc.Bacc("TRN2", target_bir_lowering=False, num_devices=1)
    arrays = {name: np.ascontiguousarray(a) for name, a in arrays.items()}
    ins = {name: nc.dram_tensor(f"in_{name}", a.shape, mybir.dt.from_np(a.dtype), kind="ExternalInput").ap()
           for name, a in arrays.items()}
    out = nc.dram_tensor("out", (B, T, D), F32, kind="ExternalOutput").ap()
    program(nc, ins, out)
    run = run_bass_kernel_spmd(nc, [{f"in_{name}": a for name, a in arrays.items()}], core_ids=[0])
    return run.results[0]["out"]
```

```python
from contextlib import ExitStack

import concourse.bass as bass
from concourse import mybir

F32 = mybir.dt.float32
F32R = mybir.dt.float32r
U32 = mybir.dt.uint32
ALU = mybir.AluOpType
ACT = mybir.ActivationFunctionType
AX = mybir.AxisListType

B = 8
T = 512
D = 256
C = 128
P = 128
QT = T // P
DH = D // P
HEADS = 16
E = 8
DK = D // HEADS
PACKS = 4
HP = HEADS // PACKS
SLABS = HEADS // 2
S_BANKS, T_BANKS, M_BANKS = 2, 2, 3
A_AT, PV_AT = 1, 1
LN_EPS = 1e-5
RMS_EPS = 1e-6


def cross_attention(nc, x, ctxT, g_xattn, wq, bq, wk, bk, wv, bv, wo, bo, identity, key_rows, x1):
    with ExitStack() as ctx:
        def sb(name, shape, dt=F32):
            return ctx.enter_context(nc.sbuf_tensor("xa_" + name, shape, dt))

        def psum(name, shape):
            return ctx.enter_context(nc.psum_tensor("xa_" + name, shape, F32))

        def sem(name):
            return ctx.enter_context(nc.semaphore("xa_" + name))

        ident = sb("ident", [P, P])
        wq_sb = sb("wq", [P, DH, D])
        wk_sb = sb("wk", [P, D])
        wv_sb = sb("wv", [P, D])
        wo_sb = sb("wo", [P, DH, D])
        bq_sb = sb("bq", [P, DH])
        bk_sb = sb("bk", [P, DH])
        bv_sb = sb("bv", [P, D])
        bo_sb = sb("bo", [P, D])
        gate = sb("gate", [P, 1])
        gated_bo = sb("gated_bo", [P, D])
        tick = sb("tick", [P, 16])
        veps_tick = sb("veps_tick", [P, 1])
        neg_half = sb("neg_half", [P, QT])
        key_init = sb("key_init", [P, 2, T])

        xt = sb("xt", [P, QT, D])
        ctx_sb = sb("ctx", [P, T])
        stats = sb("stats", [P, QT, 6])
        mv = sb("mv", [P, QT, 2])
        veps = sb("veps", [P, QT])
        rstd = sb("rstd", [P, QT])
        xn = sb("xn", [P, QT, D])
        xnT = sb("xnT", [P, DH, T])
        q_hi = sb("q_hi", [P, DH, T], F32R)
        q_lo = sb("q_lo", [P, DH, T], F32R)
        k_hi = sb("k_hi", [P, DH, T], F32R)
        k_lo = sb("k_lo", [P, DH, T], F32R)
        v_new = sb("v_new", [P, QT, D])
        v_aug = sb("v_aug", [P, QT, HEADS, 2 * DK])
        q_slab = sb("q_slab", [P, SLABS, T], F32R)
        k_slab = sb("k_slab", [P, HEADS, T], F32R)
        q_words = q_slab[:, :, :].bitcast(F32)
        k_words = k_slab[:, :, :].bitcast(F32)
        row_max = sb("row_max", [P, 2, QT, HP])
        m_hi = sb("m_hi", [HP, T], F32R)
        m_lo = sb("m_lo", [HP, T], F32R)
        probs = sb("probs", [P, 8, T])
        o_pack = sb("o_pack", [P, PACKS, T])
        r_sum = sb("r_sum", [P, QT, HEADS])
        o_tok = sb("o_tok", [P, QT, D])
        oT = sb("oT", [P, DH, T])
        x_res = sb("x_res", [P, QT, D])
        x_bias = sb("x_bias", [P, QT, D])
        x1_sb = sb("x1_sb", [P, QT, D])

        ps_s = psum("ps_s", [P, S_BANKS, T])
        ps_t = psum("ps_t", [P, T_BANKS, T])
        ps_o = psum("ps_o", [P, T])
        ps_m = psum("ps_m", [P, M_BANKS, T])

        consts = sem("consts")
        gp_set = sem("gp_set")
        gate_ready = sem("gate_ready")
        gbo_ready = sem("gbo_ready")
        slabs_set = sem("slabs_set")
        x_loaded = sem("x_loaded")
        ctx_loaded = sem("ctx_loaded")
        xres_loaded = sem("xres_loaded")
        stat_done = sem("stat_done")
        mv_done = sem("mv_done")
        rstd_step = sem("rstd_step")
        xn_ready = sem("xn_ready")
        xT_turned = sem("xT_turned")
        xT_copied = sem("xT_copied")
        q_done = sem("q_done")
        q_hi_ready = sem("q_hi_ready")
        q_lo_ready = sem("q_lo_ready")
        k_done = sem("k_done")
        k_hi_ready = sem("k_hi_ready")
        k_lo_ready = sem("k_lo_ready")
        v_done = sem("v_done")
        v_new_ready = sem("v_new_ready")
        v_ready = sem("v_ready")
        pack_loaded = [sem(f"pack_loaded{p}") for p in range(PACKS)]
        s_ready = sem("s_ready")
        max_done = sem("max_done")
        m_turned = sem("m_turned")
        m_hi_ready = sem("m_hi_ready")
        m_lo_ready = sem("m_lo_ready")
        m_loaded = [sem(f"m_loaded{i}") for i in range(2)]
        st_ready = sem("st_ready")
        exp_done = sem("exp_done")
        pv_done = sem("pv_done")
        o_copied = sem("o_copied")
        o_turned = sem("o_turned")
        r_done = sem("r_done")
        o_normed = sem("o_normed")
        oT_turned = sem("oT_turned")
        oT_copied = sem("oT_copied")
        out_done = sem("out_done")
        xbias_ready = sem("xbias_ready")
        x1_ready = sem("x1_ready")
        x1_stored = sem("x1_stored")

        x_v = x.rearrange("b (t p) d -> b p t d", p=P)
        x1_v = x1.rearrange("b (t p) d -> b p t d", p=P)

        def one(ap, b):
            return ap[bass.ds(b, 1)].rearrange("o p t d -> p (o t) d")

        PACK_LOAD = 9 * 16
        MAX_LOAD = 4 * 16
        TASKS = {(0, "A"): [("m", 0)], (0, "B"): [("O", 0)], (1, "A"): [("O", 1)],
                 (1, "B"): [("O", 2)], (2, "A"): [("O", 3)], (2, "B"): [("K", 0), ("X", 0)],
                 (3, "B"): [("X", 1), ("m", 1)], (4, "B"): [("Q", 0), ("K", 1)], (5, "B"): [("Q", 1)],
                 (6, "A"): [("T", 0)], (6, "B"): [("T", 1)], (7, "A"): [("W", 0)],
                 (7, "B"): [("W", 1), ("m", 2)], (8, "A"): [("V", 0)], (8, "B"): [("V", 1)],
                 (11, "B"): [("m", 3)]}
        NORM_AT = 2
        FRONT, TAIL = "XKQV", "OTW"

        def tasks(b, k, place, first, last):
            for kind, i in TASKS.get((k, place), []):
                if kind in FRONT and not last:
                    yield kind, i, b + 1
                elif kind in TAIL and not first:
                    yield kind, i, b - 1
                elif kind == "m" and not (last and i == 3):
                    yield kind, i, 4 * b + i + 1

        PLACES = [(k, place) for k in range(16) for place in "AB"]
        ORDER = [t for place in PLACES for t in TASKS.get(place, [])]

        def bank(kind, i):
            return ps_m[:, ORDER.index((kind, i)) % M_BANKS, :]

        def tasks_before(b, k, place, first, last):
            at = PLACES.index((k, place))
            return tasks(b, *PLACES[at - 1], first, last) if at else ()

        def freed(kind, i, b):
            return {"X": [(xT_copied, 2 * b + i + 1)], "K": [(k_hi_ready, 2 * b + i + 1), (k_lo_ready, 2 * b + i + 1)],
                    "Q": [(q_hi_ready, 2 * b + i + 1), (q_lo_ready, 2 * b + i + 1)], "V": [(v_new_ready, 2 * b + i + 1)],
                    "O": [(o_normed, 4 * b + i + 1)], "T": [(oT_copied, 2 * b + i + 1)], "W": [(x1_ready, 2 * b + i + 1)],
                    "m": [(m_hi_ready, b + 1), (m_lo_ready, b + 1)]}[kind]

        def before(b, k, place, kind, i, first, last):
            mine = ORDER.index((kind, i)) % M_BANKS
            for kk, pl in reversed(PLACES[:PLACES.index((k, place))]):
                for t in tasks(b, kk, pl, first, last):
                    if ORDER.index(t[:2]) % M_BANKS == mine:
                        return t
            kind, i = [t for t in ORDER if ORDER.index(t) % M_BANKS == mine][-1]
            return kind, i, 4 * b if kind == "m" else b

        block = ctx.enter_context(nc.Block())

        @block.sync
        def _(sp):
            def load_x(b, first=False):
                if not first:
                    sp.wait_ge(xn_ready, QT * b)
                sp.dma_start(xt[:, :, :], one(x_v, b)).then_inc(x_loaded, 16)
                if not first:
                    sp.wait_ge(v_done, 2 * b)
                sp.dma_start(ctx_sb[:, :], ctxT[bass.ds(b, 1)].rearrange("o p t -> p (o t)")).then_inc(ctx_loaded, 16)

            load_x(0, True)
            for dst, src in ((ident, identity), (wk_sb, wk), (wv_sb, wv)):
                sp.dma_start(dst[:, :], src).then_inc(consts, 16)
            sp.dma_start(key_init[:, :, :], key_rows).then_inc(consts, 16)
            for dst, src in ((wq_sb, wq), (wo_sb, wo)):
                sp.dma_start(dst[:, :, :], src.rearrange("(h p) n -> p h n", p=P)).then_inc(consts, 16)
            for dst, src in ((bq_sb, bq), (bk_sb, bk)):
                sp.dma_start(dst[:, :], src).then_inc(consts, 16)
            for dst, src in ((bv_sb, bv), (bo_sb, bo), (gate, g_xattn)):
                sp.dma_start(dst[:, :], src.partition_broadcast(P)).then_inc(consts, 16)

            def load_pack(b, p, first=False):
                if first and p == 0:
                    sp.wait_ge(slabs_set, 3)
                if p == 0:
                    for split in (k_hi_ready, k_lo_ready):
                        sp.wait_ge(split, 2 * b + 2)
                if not first:
                    sp.wait_ge(st_ready, 64 * b - 64 + 16 * p + 16)
                for r, ks in enumerate((k_hi, k_lo, k_hi)):
                    for a in range(2):
                        lo = 32 * p + DK * a
                        sp.dma_start(k_words[32 * r + DK * a:32 * r + DK * a + DK, HP * p + a:HP * p + HP:2, :],
                                     ks[lo:lo + DK, :, :].bitcast(F32)).then_inc(pack_loaded[p], 16)
                if p == 0:
                    for split in (q_hi_ready, q_lo_ready):
                        sp.wait_ge(split, 2 * b + 2)
                for r, qs in enumerate((q_hi, q_hi, q_lo)):
                    sp.dma_start(q_words[32 * r:32 * r + 32, 2 * p:2 * p + 2, :], qs[32 * p:32 * p + 32, :, :].bitcast(F32))\
                      .then_inc(pack_loaded[p], 16)

            def load_max(n, p, first=False):
                sp.wait_ge(m_hi_ready, n + 1)
                sp.wait_ge(m_lo_ready, n + 1)
                if not first:
                    sp.wait_ge(st_ready, 16 * n - 48)
                for r, m in ((96, m_hi), (98, m_lo)):
                    for i in range(2):
                        sp.dma_start(q_words[r:r + 2, 2 * p + i, :], m[2 * i:2 * i + 2, :].bitcast(F32))\
                          .then_inc(m_loaded[p % 2], 16)

            def body(b, first=False, last=False):
                if not last:
                    load_x(b + 1)
                load_max(4 * b + 1, 1, first)
                if not first:
                    load_pack(b, 3)
                    sp.wait_ge(xbias_ready, b - 1)
                    sp.dma_start(x_res[:, :, :], one(x_v, b - 1)).then_inc(xres_loaded, 16)
                load_max(4 * b + 2, 2, first)
                if not last:
                    load_pack(b + 1, 0)
                if not first:
                    sp.wait_ge(x1_ready, 2 * b)
                    sp.dma_start(one(x1_v, b - 1), x1_sb[:, :, :]).then_inc(x1_stored, 16)
                load_max(4 * b + 3, 3, first)
                if not last:
                    load_pack(b + 1, 1)
                    load_max(4 * b + 4, 0)
                    load_pack(b + 1, 2)

            for p in range(PACKS):
                load_pack(0, p, True)
            load_max(0, 0, True)
            body(0, first=True)
            with sp.Fori(1, B - 1) as b:
                body(b)
            body(B - 1, last=True)
            sp.wait_ge(xbias_ready, B - 1)
            sp.dma_start(x_res[:, :, :], one(x_v, B - 1)).then_inc(xres_loaded, 16)
            sp.wait_ge(x1_ready, 2 * B)
            sp.dma_start(one(x1_v, B - 1), x1_sb[:, :, :]).then_inc(x1_stored, 16)
            sp.wait_ge(x1_stored, 16 * B)

        @block.gpsimd
        def _(pool):
            pool.memset(neg_half[:, :], -0.5).then_inc(gp_set, 1)
            pool.memset(v_aug[:, :, :, :], 1.0).then_inc(gp_set, 1)
            pool.memset(tick[:, :], 0.0).then_inc(gp_set, 1)
            pool.wait_ge(gp_set, 3)

            def bear_wait(n):
                pool.tensor_tensor(tick[:, n:n + 1], tick[:, 0:1], tick[:, 0:1], ALU.add)

            def deviation(b, first=False):
                pool.wait_ge(mv_done, QT * b + QT)
                if not first:
                    pool.wait_ge(xn_ready, QT * b)
                bear_wait(1)
                pool.tensor_scalar(veps[:, :], mv[:, :, 1], LN_EPS, None, ALU.add).then_inc(rstd_step, 1)
                pool.wait_ge(rstd_step, 2 * b + 1)
                pool.tensor_tensor(rstd[:, :], veps[:, :], neg_half[:, :], ALU.pow).then_inc(rstd_step, 1)

            def add_bias(b):
                pool.wait_ge(xres_loaded, 16 * b + 16)
                pool.wait_ge(x1_ready, 2 * b)
                for t in range(QT):
                    ins = pool.tensor_tensor(x_bias[:, t, :], x_res[:, t, :], gated_bo[:, :], ALU.add)
                ins.then_inc(xbias_ready, 1)

            def place_v(b, c, first=False):
                pool.wait_ge(v_new_ready, 2 * b + c // 2 + 1)
                if not first:
                    pool.wait_ge(pv_done, 16 * b - 3 + c)
                bear_wait(3 + c)
                pool.tensor_copy(v_aug[:, c, :, 0:DK],
                                 v_new[:, c, :].rearrange("p (h d) -> p h d", d=DK)).then_inc(v_ready, 1)

            def body(b, first=False, last=False):
                if not last:
                    deviation(b + 1)
                if not first:
                    add_bias(b - 1)
                if not last:
                    for c in range(QT):
                        place_v(b + 1, c)

            deviation(0, True)
            pool.wait_ge(gbo_ready, 1)
            for c in range(QT):
                place_v(0, c, True)
            body(0, first=True)
            with pool.Fori(1, B - 1) as b:
                body(b)
            body(B - 1, last=True)
            add_bias(B - 1)

        @block.scalar
        def _(act):
            act.wait_ge(consts, 16 * 11)
            act.activation(gate[:, :], gate[:, :], ACT.Tanh).then_inc(gate_ready, 1)

            def task(kind, i, b, first=False):
                if kind == "X":
                    act.wait_ge(xT_turned, 2 * b + i + 1)
                    act.copy(xnT[:, i, :], bank(kind, i)).then_inc(xT_copied, 1)
                elif kind in "QK":
                    done, hi, bias, ready = ((q_done, q_hi, bq_sb, q_hi_ready), (k_done, k_hi, bk_sb, k_hi_ready))[kind == "K"]
                    act.wait_ge(done, 2 * b + i + 1)
                    if not first:
                        for p in range(PACKS):
                            act.wait_ge(pack_loaded[p], PACK_LOAD * b)
                    act.activation(hi[:, i, :], bank(kind, i), ACT.Identity, bias=bias[:, i:i + 1]).then_inc(ready, 1)
                elif kind == "m":
                    act.wait_ge(m_turned, b + 1)
                    if not first:
                        act.wait_ge(m_loaded[i % 2], MAX_LOAD * ((b - i - 1) // 2 + i // 2 + 1))
                    act.mul(m_hi[:, :], bank(kind, i)[0:HP, :], -1.0).then_inc(m_hi_ready, 1)
                elif kind == "T":
                    act.wait_ge(oT_turned, 2 * b + i + 1)
                    act.copy(oT[:, i, :], bank(kind, i)).then_inc(oT_copied, 1)

            def exp(b, k, h, first=False):
                i = HP * k + h
                act.wait_ge(st_ready, 64 * b + i + 1)
                if not (first and i < 8):
                    act.wait_ge(pv_done, 16 * b + k - 1)
                act.activation(probs[:, i % 8, :], ps_t[:, i % T_BANKS, :], ACT.Exp, scale=DK ** -0.5).then_inc(exp_done, 1)

            def copy_o(b, p, first=False):
                act.wait_ge(pv_done, 16 * b + 4 * p + 4)
                if not first:
                    act.wait_ge(o_turned, 4 * b)
                act.copy(o_pack[:, p, :], ps_o[:, :]).then_inc(o_copied, 1)

            def body(b, first=False, last=False):
                for k in range(16):
                    exp(b, k, 0, first)
                    for t in tasks(b, k, "A", first, last):
                        task(*t)
                    for h in range(1, HP):
                        exp(b, k, h, first)
                    if k % 4 == 0 and k > 0:
                        copy_o(b, k // 4 - 1, first)
                    if k == 0 and not first:
                        copy_o(b - 1, 3, True)
                    for t in tasks(b, k, "B", first, last):
                        task(*t)

            act.copy(k_slab[:, 1::2, :], key_init[:, 1:2, :].broadcast_to([P, HEADS // 2, T])).then_inc(slabs_set, 1)
            for i in range(2):
                task("X", i, 0)
            for i in range(2):
                task("K", i, 0, True)
                task("Q", i, 0, True)
            task("m", 3, 0, True)
            body(0, first=True)
            with act.Fori(1, B - 1) as b:
                body(b)
            body(B - 1, last=True)
            copy_o(B - 1, 3, True)
            for i in range(2):
                task("T", i, B - 1)

        @block.vector
        def _(dve):
            def statistics(b, first=False):
                dve.wait_ge(x_loaded, 16 * b + 16)
                if not first:
                    dve.wait_ge(rstd_step, 2 * b)
                for t in range(QT):
                    dve.bn_stats(stats[:, t, :], xt[:, t, :]).then_inc(stat_done, 1)
                dve.wait_ge(stat_done, QT * b + QT)
                dve.tensor_copy(veps_tick[:, 0:1], stats[:, 0, 0:1])
                for t in range(QT):
                    dve.bn_aggr(mv[:, t, :], stats[:, t, :]).then_inc(mv_done, 1)

            def normalize(b, first=False):
                dve.wait_ge(rstd_step, 2 * b + 2)
                if not first:
                    dve.wait_ge(xT_turned, 2 * b)
                for t in range(QT):
                    dve.tensor_scalar(xn[:, t, :], xt[:, t, :], mv[:, t, 0:1], rstd[:, t:t + 1],
                                      ALU.subtract, ALU.mult).then_inc(xn_ready, 1)

            def task(kind, i, b, first=False):
                if kind in "QK":
                    done, hi, lo, bias, h_ready, l_ready = (
                        (q_done, q_hi, q_lo, bq_sb, q_hi_ready, q_lo_ready),
                        (k_done, k_hi, k_lo, bk_sb, k_hi_ready, k_lo_ready))[kind == "K"]
                    dve.wait_ge(h_ready, 2 * b + i + 1)
                    dve.scalar_tensor_tensor(out=lo[:, i, :], in0=bank(kind, i), scalar=bias[:, i:i + 1],
                                             in1=hi[:, i, :].bitcast(F32), op0=ALU.add, op1=ALU.subtract)\
                       .then_inc(l_ready, 1)
                elif kind == "m":
                    dve.wait_ge(m_hi_ready, b + 1)
                    dve.scalar_tensor_tensor(out=m_lo[:, :], in0=bank(kind, i)[0:HP, :], scalar=-1.0,
                                             in1=m_hi[:, :].bitcast(F32), op0=ALU.mult, op1=ALU.subtract)\
                       .then_inc(m_lo_ready, 1)
                elif kind == "V":
                    dve.wait_ge(v_done, 2 * b + i + 1)
                    if not first:
                        dve.wait_ge(v_ready, QT * b)
                    dve.tensor_tensor(v_new[:, 2 * i:2 * i + 2, :], bank(kind, i).rearrange("p (t d) -> p t d", d=D),
                                      bv_sb[:, :].unsqueeze(1).broadcast_to([P, 2, D]), ALU.add).then_inc(v_new_ready, 1)
                elif kind == "O":
                    o = bank(kind, i).rearrange("p (h e) -> p h e", e=2 * DK)
                    dve.wait_ge(o_turned, 4 * b + i + 1)
                    dve.reciprocal(r_sum[:, i, :], o[:, :, DK]).then_inc(r_done, 1)
                    dve.wait_ge(r_done, 4 * b + i + 1)
                    dve.tensor_tensor(o_tok[:, i, :].rearrange("p (h d) -> p h d", d=DK), o[:, :, 0:DK],
                                      r_sum[:, i, :].unsqueeze(2).broadcast_to([P, HEADS, DK]), ALU.mult)\
                       .then_inc(o_normed, 1)
                elif kind == "W":
                    dve.wait_ge(out_done, 2 * b + i + 1)
                    dve.wait_ge(xbias_ready, b + 1)
                    dve.wait_ge(x1_stored, 16 * b)
                    dve.scalar_tensor_tensor(out=x1_sb[:, 2 * i:2 * i + 2, :].rearrange("p t d -> p (t d)"), in0=bank(kind, i),
                                             scalar=gate[:, 0:1],
                                             in1=x_bias[:, 2 * i:2 * i + 2, :].rearrange("p t d -> p (t d)"),
                                             op0=ALU.mult, op1=ALU.add).then_inc(x1_ready, 1)

            def row_maximum(n, par, c, t, first=False):
                i = 4 * c + t
                dve.wait_ge(s_ready, 16 * n + i + 1)
                if i == 0 and not first:
                    dve.wait_ge(m_turned, n - 1)
                dve.tensor_reduce(row_max[:, par, t, c:c + 1], ps_s[:, i % S_BANKS, :], AX.X, ALU.max).then_inc(max_done, 1)

            def body(b, first=False, last=False):
                for k in range(16):
                    p, c = k // 4, k % 4
                    if k == 1 and not last:
                        statistics(b + 1)
                    if k == NORM_AT and not last:
                        normalize(b + 1)
                    scores = not (last and p >= 2)
                    for t in range(2 * scores):
                        row_maximum(4 * b + p + 2, p % 2, c, t)
                    for t in tasks_before(b, k, "A", first, last):
                        task(*t)
                    for t in range(2, 2 + 2 * scores):
                        row_maximum(4 * b + p + 2, p % 2, c, t)
                    for t in tasks_before(b, k, "B", first, last):
                        task(*t)

            statistics(0, True)
            normalize(0, True)
            dve.wait_ge(consts, 16 * 11)
            dve.tensor_copy(q_slab[:, :, :], key_init[:, 0:1, :].broadcast_to([P, SLABS, T])).then_inc(slabs_set, 1)
            dve.tensor_copy(k_slab[:, 0::2, :], key_init[:, 0:1, :].broadcast_to([P, HEADS // 2, T])).then_inc(slabs_set, 1)
            dve.wait_ge(gate_ready, 1)
            dve.tensor_scalar(gated_bo[:, :], bo_sb[:, :], gate[:, 0:1], None, ALU.mult).then_inc(gbo_ready, 1)
            for i in range(2):
                task("K", i, 0)
                task("Q", i, 0)
            for i in range(2):
                task("V", i, 0, True)
            for n in range(2):
                for c in range(HP):
                    for t in range(QT):
                        row_maximum(n, n, c, t, True)
                if n == 0:
                    task("m", 3, 0)
            body(0, first=True)
            with dve.Fori(1, B - 1) as b:
                body(b)
            body(B - 1, last=True)
            for i in range(QT):
                task("O", i, B - 1)
            for i in range(2):
                task("W", i, B - 1)

        @block.tensor
        def _(pe):
            pe.wait_ge(consts, 16 * 11)

            def task(kind, i, b, prev):
                if prev is not None:
                    for s, v in freed(*prev):
                        pe.wait_ge(s, v)
                ps = bank(kind, i)
                if kind == "X":
                    if i == 0:
                        pe.wait_ge(xn_ready, QT * b + QT)
                    for t in range(QT):
                        mm = pe.transpose(ps[:, t * P:(t + 1) * P], xn[:, t, i * P:(i + 1) * P], ident[:, :])
                    mm.then_inc(xT_turned, 1)
                elif kind == "Q":
                    pe.wait_ge(xT_copied, 2 * b + 2)
                    for h in range(DH):
                        mm = pe.matmul(ps, wq_sb[:, h, i * P:(i + 1) * P], xnT[:, h, :],
                                       start=(h == 0), stop=(h == DH - 1))
                    mm.then_inc(q_done, 1)
                elif kind == "K":
                    pe.wait_ge(ctx_loaded, 16 * b + 16)
                    pe.matmul(ps, wk_sb[:, i * P:(i + 1) * P], ctx_sb[:, :], start=True, stop=True)\
                      .then_inc(k_done, 1)
                elif kind == "V":
                    for t in range(2 * i, 2 * i + 2):
                        mm = pe.matmul(ps[:, (t % 2) * D:(t % 2 + 1) * D], ctx_sb[:, t * P:(t + 1) * P], wv_sb[:, :],
                                       start=True, stop=True)
                    mm.then_inc(v_done, 1)
                elif kind == "m":
                    pe.wait_ge(max_done, 16 * b + 16)
                    for t in range(QT):
                        mm = pe.transpose(ps[0:HP, t * P:(t + 1) * P], row_max[:, (i + 1) % 2, t, :], ident[:, :])
                    mm.then_inc(m_turned, 1)
                elif kind == "O":
                    pe.wait_ge(o_copied, 4 * b + 4)
                    for p in range(PACKS):
                        mm = pe.transpose(ps[:, p * P:(p + 1) * P], o_pack[:, p, i * P:(i + 1) * P], ident[:, :])
                    mm.then_inc(o_turned, 1)
                elif kind == "T":
                    if i == 0:
                        pe.wait_ge(o_normed, 4 * b + 4)
                    for t in range(QT):
                        mm = pe.transpose(ps[:, t * P:(t + 1) * P], o_tok[:, t, i * P:(i + 1) * P], ident[:, :])
                    mm.then_inc(oT_turned, 1)
                elif kind == "W":
                    if i == 0:
                        pe.wait_ge(oT_copied, 2 * b + 2)
                    for t in range(2 * i, 2 * i + 2):
                        for h in range(DH):
                            mm = pe.matmul(ps[:, (t % 2) * D:(t % 2 + 1) * D], oT[:, h, t * P:(t + 1) * P],
                                           wo_sb[:, h, :], start=(h == 0), stop=(h == DH - 1))
                    mm.then_inc(out_done, 1)

            def max_scores(n, p, c, t, b, first=False):
                i = 4 * c + t
                if i == 0:
                    pe.wait_ge(pack_loaded[p], PACK_LOAD * (b + 1))
                if not (first and i < S_BANKS):
                    last = i - S_BANKS if i >= S_BANKS else i + (16 - i - 1) // S_BANKS * S_BANKS - 16
                    pe.wait_ge(max_done, 16 * n + last + 1)
                pe.matmul(ps_s[:, i % S_BANKS, :], q_slab[0:96, 2 * p + c // 2, t * P:(t + 1) * P],
                          k_slab[0:96, HP * p + c, :], start=True, stop=True).then_inc(s_ready, 1)

            def exp_scores(b, p, c, h, first=False):
                i = 16 * p + HP * c + h
                if c == 0 and h == 0:
                    pe.wait_ge(m_loaded[p % 2], MAX_LOAD * (2 * b + p // 2 + 1))
                if not (first and i < T_BANKS):
                    pe.wait_ge(exp_done, 64 * b + i - T_BANKS + 1)
                pe.matmul(ps_t[:, i % T_BANKS, :], k_slab[0:100, HP * p + h, c * P:(c + 1) * P],
                          q_slab[0:100, 2 * p + h // 2, :], start=True, stop=True).then_inc(st_ready, 1)

            def weigh_values(b, k, first=False):
                p, c = k // 4, k % 4
                pe.wait_ge(exp_done, 64 * b + HP * k + HP)
                if p == 0:
                    pe.wait_ge(v_ready, QT * b + c + 1)
                if c == 0 and not (first and p == 0):
                    pe.wait_ge(o_copied, 4 * b + p)
                for j in range(HP):
                    mm = pe.matmul(ps_o[32 * j:32 * j + 32, :], v_aug[:, c, HP * p + j, :],
                                   probs[:, (HP * k + j) % 8, :], start=(c == 0), stop=(c == QT - 1),
                                   skip_group_check=True)
                mm.then_inc(pv_done, 1)

            def body(b, first=False, last=False):
                for k in range(16):
                    p, c = k // 4, k % 4
                    n, sp_, sb_ = 4 * b + p + 2, (p + 2) % PACKS, b + (p + 2) // PACKS
                    scores = not (last and p >= 2)
                    for h in range(HP):
                        if scores:
                            max_scores(n, sp_, c, h, sb_)
                        if h == A_AT:
                            for t in tasks(b, k, "A", first, last):
                                task(*t, before(b, k, "A", *t[:2], first, last))
                        exp_scores(b, p, c, h, first)
                        if h == PV_AT and k > 0:
                            weigh_values(b, k - 1, first)
                        elif h == PV_AT and not first:
                            weigh_values(b - 1, 15)
                    for t in tasks(b, k, "B", first, last):
                        task(*t, before(b, k, "B", *t[:2], first, last))

            had = {}

            def in_turn(kind, i, b):
                at = ORDER.index((kind, i)) % M_BANKS
                task(kind, i, b, had.get(at))
                had[at] = (kind, i, b)

            for kind, i in (("X", 0), ("X", 1), ("K", 0), ("Q", 0), ("K", 1), ("Q", 1), ("V", 0), ("V", 1)):
                in_turn(kind, i, 0)
            for n in range(2):
                for c in range(HP):
                    for t in range(QT):
                        max_scores(n, n, c, t, 0, n == 0)
                if n == 0:
                    in_turn("m", 3, 0)
            body(0, first=True)
            with pe.Fori(1, B - 1) as b:
                body(b)
            body(B - 1, last=True)
            weigh_values(B - 1, 15)
            for place in PLACES:
                for t in tasks(B - 1, *place, False, True):
                    had[ORDER.index(t[:2]) % M_BANKS] = t
            for kind, i in [("O", i) for i in range(QT)] + [("T", i) for i in range(2)] + [("W", i) for i in range(2)]:
                in_turn(kind, i, B - 1)


KC = D // 4
H2 = D // KC


def self_attention(nc, x1, g_ffn, g1, wqT, wkvT, woT, g2, wrT, identity, key_rows, x_norm, base, x_moe,
                   x_tok, logits):
    with ExitStack() as ctx:
        def sb(name, shape, dt=F32):
            return ctx.enter_context(nc.sbuf_tensor("sa_" + name, shape, dt))

        def psum(name, shape):
            return ctx.enter_context(nc.psum_tensor("sa_" + name, shape, F32))

        def sem(name):
            return ctx.enter_context(nc.semaphore("sa_" + name))

        ident = sb("ident", [P, P])
        wq_sb = sb("wq", [P, DH, D])
        wkv_sb = sb("wkv", [P, DH, 2 * KC])
        wo_sb = sb("wo", [P, DH, D])
        wr_sb = sb("wr", [P, DH, E])
        g1_sb = sb("g1", [P, DH])
        g2_sb = sb("g2", [P, DH])
        gate = sb("gate", [P, 1])
        tick = sb("tick", [P, 16])
        veps_tick = sb("veps_tick", [P, 1])
        neg_half = sb("neg_half", [P, QT])
        ones = sb("ones", [P, 32])
        key_init = sb("key_init", [P, 2, T])

        xt = sb("xt", [P, QT, D])
        stats = sb("stats", [P, QT, 6])
        mv = sb("mv", [P, QT, 2])
        r_small = sb("r_small", [P, 6, QT])
        xf = sb("xf", [P, QT, D])
        xn = sb("xn", [P, QT, D])
        xnT = sb("xnT", [P, DH, T])
        q_hi = sb("q_hi", [P, DH, T], F32R)
        q_lo = sb("q_lo", [P, DH, T], F32R)
        k_hi = sb("k_hi", [KC, T], F32R)
        k_lo = sb("k_lo", [KC, T], F32R)
        vT = sb("vT", [P, T])
        values = sb("values", [P, 2, QT, KC])
        q_a = sb("q_a", [P, 2, H2, T], F32R)
        q_b = sb("q_b", [P, 2, H2, T], F32R)
        k_a = sb("k_a", [P, 2, T], F32R)
        k_b0 = sb("k_b0", [P, 2, T], F32R)
        k_b1 = sb("k_b1", [P, 2, T], F32R)
        words = {n: t for n, t in (("q_a", q_a[:, :, :, :].bitcast(F32)), ("q_b", q_b[:, :, :, :].bitcast(F32)),
                                   ("k_a", k_a[:, :, :].bitcast(F32)), ("k_b0", k_b0[:, :, :].bitcast(F32)),
                                   ("k_b1", k_b1[:, :, :].bitcast(F32)))}
        row_max = sb("row_max", [P, QT, H2])
        m_hi = sb("m_hi", [H2, T], F32R)
        m_lo = sb("m_lo", [H2, T], F32R)
        probs = sb("probs", [P, 8, T])
        o_pair = sb("o_pair", [P, 2, T])
        sums = sb("sums", [P, T])
        r_sum = sb("r_sum", [P, QT, H2])
        o_tok = sb("o_tok", [P, QT, D])
        oT = sb("oT", [P, DH, T])
        x1_res = sb("x1_res", [P, QT, D])
        xf_res = sb("xf_res", [P, QT, D])
        x2 = sb("x2", [P, QT, D])
        squares = sb("squares", [P, D])
        sq_sum = sb("sq_sum", [P, QT])
        rms2 = sb("rms2", [P, 2, QT])
        xn2 = sb("xn2", [P, QT, D])
        base_sb = sb("base_sb", [P, QT, D])
        moeT = sb("moeT", [P, DH, T])

        logits_sb = sb("logits", [P, QT * E])

        ps_s = psum("ps_s", [P, 2, T])
        ps_t = psum("ps_t", [P, 2, T])
        ps_o = psum("ps_o", [P, 2, T])
        ps_r = psum("ps_r", [P, T])
        ps_m = psum("ps_m", [P, T])

        consts = sem("consts")
        set_up = sem("set_up")
        gp_set = sem("gp_set")
        gate_ready = sem("gate_ready")
        x_loaded = sem("x_loaded")
        res_loaded = sem("res_loaded")
        stat_done = sem("stat_done")
        mv_done = sem("mv_done")
        r_step = sem("r_step")
        xf_ready = sem("xf_ready")
        xn_ready = sem("xn_ready")
        xf_stored = sem("xf_stored")
        xT_turned = sem("xT_turned")
        xT_copied = sem("xT_copied")
        kv_done = sem("kv_done")
        k_hi_ready = sem("k_hi_ready")
        k_lo_ready = sem("k_lo_ready")
        vT_ready = sem("vT_ready")
        q_done = sem("q_done")
        q_hi_ready = sem("q_hi_ready")
        q_lo_ready = sem("q_lo_ready")
        v_turned = sem("v_turned")
        v_ready = sem("v_ready")
        slabs_loaded = [[sem(f"slabs_loaded{i}{a}") for a in range(2)] for i in range(2)]
        s_ready = sem("s_ready")
        max_done = sem("max_done")
        m_turned = sem("m_turned")
        m_hi_ready = sem("m_hi_ready")
        m_lo_ready = sem("m_lo_ready")
        m_loaded = sem("m_loaded")
        st_ready = sem("st_ready")
        exp_done = sem("exp_done")
        pv_done = sem("pv_done")
        o_copied = sem("o_copied")
        o_turned = sem("o_turned")
        r_done = sem("r_done")
        o_normed = sem("o_normed")
        oT_turned = sem("oT_turned")
        oT_copied = sem("oT_copied")
        out_done = sem("out_done")
        x2_ready = sem("x2_ready")
        sq_done = sem("sq_done")
        rms_step = sem("rms_step")
        xn2_ready = sem("xn2_ready")
        base_ready = sem("base_ready")
        base_stored = sem("base_stored")
        moe_turned = sem("moe_turned")
        moe_ready = sem("moe_ready")
        moe_stored = sem("moe_stored")

        tok_stored = sem("tok_stored")
        logits_done = sem("logits_done")
        logits_copied = sem("logits_copied")
        logits_stored = sem("logits_stored")

        def rows(ap, b):
            return ap.rearrange("b (t p) d -> b p t d", p=P)[bass.ds(b, 1)].rearrange("o p t d -> p (o t) d")

        SLAB_LOAD = 7 * 16, 3 * 16
        HEAD_ORDER = 0, 2, 1, 3
        MAX_LOAD = 2 * H2 * 16
        TASKS = {(0, 2): ["Y0"], (0, 3): ["Y1", "O0"], (1, 0): ["V"], (1, 1): ["O1"], (1, 2): ["O2"],
                 (1, 3): ["O3"], (2, 0): ["T0", "X0"], (2, 1): ["T1", "X1"], (2, 2): ["W0"], (2, 3): ["M"],
                 (3, 1): ["W1", "K"], (3, 2): ["Q0"], (3, 3): ["Q1", "L"]}
        AHEAD = {"X": 2, "K": 2, "Q": 2, "V": 1, "M": 1, "O": -1, "T": -1, "W": -1, "Y": -2, "L": -2}

        SPARE = {("Y", 0): 0, ("Y", 1): 1, ("K", 0): 0, ("Q", 0): 1, ("Q", 1): 0}

        def bank(kind, i):
            return ps_s[:, SPARE[kind, i], :] if (kind, i) in SPARE else ps_m[:, :]

        def tasks(b, place, lo, hi):
            for name in TASKS.get(place, []):
                if lo <= AHEAD[name[0]] <= hi:
                    yield name[0], int(name[1:] or 0), b + AHEAD[name[0]]

        def freed(kind, i, b):
            return {"X": [(xT_copied, 2 * b + i + 1)], "K": [(k_hi_ready, b + 1), (k_lo_ready, b + 1), (vT_ready, b + 1)],
                    "Q": [(q_hi_ready, 2 * b + i + 1), (q_lo_ready, 2 * b + i + 1)], "V": [(v_ready, b + 1)],
                    "M": [(m_hi_ready, b + 1), (m_lo_ready, b + 1)], "O": [(o_normed, QT * b + i + 1)],
                    "T": [(oT_copied, 2 * b + i + 1)], "W": [(x2_ready, 2 * b + i + 1)],
                    "Y": [(moe_ready, 2 * b + i + 1)], "L": [(logits_copied, b + 1)]}[kind]

        PROLOGUE = [("X", 0, 0), ("X", 1, 0), ("K", 0, 0), ("Q", 0, 0), ("Q", 1, 0), ("V", 0, 0),
                    ("X", 0, 1), ("X", 1, 1), ("K", 0, 1), ("Q", 0, 1), ("Q", 1, 1)]
        EPILOGUE = [("Y", 0, B - 2), ("Y", 1, B - 2), ("L", 0, B - 2)] + [("O", i, B - 1) for i in range(QT)] + \
                   [(k, i, B - 1) for k in "TWY" for i in range(2)] + [("L", 0, B - 1)]

        def all_bodies(eng, body):
            body(0, 0, 0, 2)
            body(1, 1, -1, 2)
            with eng.Fori(2, B - 3, 2) as b:
                body(b, 0, -2, 2)
                body(b + 1, 1, -2, 2)
            body(B - 2, 0, -2, 1)
            body(B - 1, 1, -2, 0)

        block = ctx.enter_context(nc.Block())

        @block.sync
        def _(sp):
            def load_x(b):
                sp.wait_ge(xn_ready, QT * b)
                sp.wait_ge(xf_ready, QT * b)
                sp.dma_start(xt[:, :, :], rows(x1, b)).then_inc(x_loaded, 16)

            load_x(0)
            sp.dma_start(ident[:, :], identity).then_inc(consts, 16)
            sp.dma_start(key_init[:, :, :], key_rows).then_inc(consts, 16)
            for dst, src in ((wq_sb, wqT), (wkv_sb, wkvT), (wo_sb, woT), (wr_sb, wrT)):
                sp.dma_start(dst[:, :, :], src.rearrange("(h p) n -> p h n", p=P)).then_inc(consts, 16)
            sp.dma_start(g1_sb[:, :], g1).then_inc(consts, 16)
            sp.dma_start(g2_sb[:, :], g2).then_inc(consts, 16)
            sp.dma_start(gate[:, :], g_ffn.partition_broadcast(P)).then_inc(consts, 16)

            def store_xf(b):
                sp.wait_ge(xf_ready, QT * b + QT)
                sp.dma_start(rows(x_norm, b), xf[:, :, :]).then_inc(xf_stored, 16)

            def load_slabs(b, par, first=False):
                if first and par == 0:
                    sp.wait_ge(set_up, 3)
                if not first:
                    sp.wait_ge(st_ready, 16 * b - 16)
                for s, v in ((k_hi_ready, b + 1), (k_lo_ready, b + 1), (q_hi_ready, 2 * b + 2), (q_lo_ready, 2 * b + 2)):
                    sp.wait_ge(s, v)
                lo, hi = slice(0, KC), slice(KC, P)
                for dst, r, src in (("k_a", lo, k_hi), ("k_a", hi, k_hi), ("k_b0", lo, k_lo), ("k_b1", lo, k_lo)):
                    sp.dma_start(words[dst][r, par, :], src[:, :].bitcast(F32)).then_inc(slabs_loaded[par][0], 16)
                for a in range(2):
                    half = slice(KC * a, KC * a + KC)
                    for dst, r, src in (("q_a", lo, q_hi), ("q_a", hi, q_lo), ("q_b", lo, q_hi)):
                        sp.dma_start(words[dst][r, par, a::2, :], src[half, :, :].bitcast(F32))\
                          .then_inc(slabs_loaded[par][a], 16)

            def load_max(b, par):
                sp.wait_ge(m_hi_ready, b + 1)
                sp.wait_ge(m_lo_ready, b + 1)
                for r, m in ((KC, m_hi), (KC + 1, m_lo)):
                    for h in range(H2):
                        sp.dma_start(words["q_b"][r:r + 1, par, h, :], m[h:h + 1, :].bitcast(F32)).then_inc(m_loaded, 16)

            def load_res(b):
                sp.wait_ge(xf_stored, 16 * b + 16)
                sp.wait_ge(base_ready, b)
                sp.dma_start(x1_res[:, :, :], rows(x1, b)).then_inc(res_loaded, 16)
                sp.dma_start(xf_res[:, :, :], rows(x_norm, b)).then_inc(res_loaded, 16)

            def store_base(b):
                sp.wait_ge(base_ready, b + 1)
                sp.dma_start(rows(base, b), base_sb[:, :, :]).then_inc(base_stored, 16)

            def store_tok(b):
                sp.wait_ge(xn2_ready, QT * b + QT)
                sp.dma_start(rows(x_tok, b), xn2[:, :, :]).then_inc(tok_stored, 16)

            def body(b, par, lo, hi):
                if hi >= 2:
                    load_x(b + 2)
                if lo <= -2:
                    store_tok(b - 2)
                if hi >= 1 and lo < 0:
                    load_slabs(b + 1, 1 - par)
                if lo < 0:
                    load_res(b - 1)
                if hi >= 2:
                    store_xf(b + 2)
                if lo < 0:
                    store_base(b - 1)
                if hi >= 1:
                    load_max(b + 1, 1 - par)

            store_xf(0)
            load_x(1)
            load_slabs(0, 0, True)
            store_xf(1)
            load_slabs(1, 1, True)
            load_max(0, 0)
            all_bodies(sp, body)
            load_res(B - 1)
            store_tok(B - 2)
            store_base(B - 1)
            store_tok(B - 1)
            sp.wait_ge(base_stored, 16 * B)
            sp.wait_ge(moe_stored, 16 * B)
            sp.wait_ge(tok_stored, 16 * B)
            sp.wait_ge(logits_stored, 16 * B)

        @block.gpsimd
        def _(pool):
            pool.memset(neg_half[:, :], -0.5).then_inc(gp_set, 1)
            pool.memset(ones[:, :], 1.0).then_inc(gp_set, 1)
            pool.memset(tick[:, :], 0.0).then_inc(gp_set, 1)
            pool.wait_ge(gp_set, 3)
            veps, rstd, square, ms, r2, both = (r_small[:, i, :] for i in range(6))

            def bear_wait(n):
                pool.tensor_tensor(tick[:, n:n + 1], tick[:, 0:1], tick[:, 0:1], ALU.add)

            def normalize(b):
                step = [0]

                def chain(ins):
                    step[0] += 1
                    ins.then_inc(r_step, 1)
                    pool.wait_ge(r_step, 7 * b + step[0])
                    bear_wait(step[0])

                pool.wait_ge(mv_done, QT * b + QT)
                bear_wait(8)
                chain(pool.tensor_scalar(veps, mv[:, :, 1], LN_EPS, None, ALU.add))
                chain(pool.tensor_tensor(rstd, veps, neg_half[:, :], ALU.pow))
                chain(pool.tensor_tensor(square, rstd, rstd, ALU.mult))
                chain(pool.tensor_tensor(ms, square, mv[:, :, 1], ALU.mult))
                chain(pool.tensor_scalar(ms, ms, RMS_EPS, None, ALU.add))
                chain(pool.tensor_tensor(r2, ms, neg_half[:, :], ALU.pow))
                chain(pool.tensor_tensor(both, r2, rstd, ALU.mult))
                pool.wait_ge(xf_stored, 16 * b)
                bear_wait(9)
                for t in range(QT):
                    pool.tensor_scalar(xf[:, t, :], xt[:, t, :], mv[:, t, 0:1], r_small[:, 1, t:t + 1],
                                       ALU.subtract, ALU.mult).then_inc(xf_ready, 1)

            def rms(b):
                pool.wait_ge(sq_done, QT * b + QT)
                bear_wait(10)
                pool.tensor_scalar(rms2[:, 0, :], sq_sum[:, :], 1.0 / D, RMS_EPS, ALU.mult, ALU.add).then_inc(rms_step, 1)
                pool.wait_ge(rms_step, 2 * b + 1)
                pool.tensor_tensor(rms2[:, 1, :], rms2[:, 0, :], neg_half[:, :], ALU.pow).then_inc(rms_step, 1)

            def body(b, par, lo, hi):
                if hi >= 2:
                    normalize(b + 2)
                if lo < 0:
                    rms(b - 1)

            normalize(0)
            normalize(1)
            all_bodies(pool, body)
            rms(B - 1)

        @block.scalar
        def _(act):
            act.wait_ge(consts, 16 * 9)
            act.activation(gate[:, :], gate[:, :], ACT.Tanh).then_inc(gate_ready, 1)

            def task(kind, i, b, par=0, first=False):
                ps = bank(kind, i)
                if kind == "X":
                    act.wait_ge(xT_turned, 2 * b + i + 1)
                    act.mul(xnT[:, i, :], ps[:, :], g1_sb[:, i:i + 1]).then_inc(xT_copied, 1)
                elif kind == "K":
                    act.wait_ge(kv_done, b + 1)
                    if not first:
                        for a in range(2):
                            act.wait_ge(slabs_loaded[1 - par][a], SLAB_LOAD[a] * ((b - 1) // 2 + 1))
                    act.wait_ge(v_turned, b)
                    act.copy(vT[:, :], ps[:, :]).then_inc(vT_ready, 1)
                    act.copy(k_hi[:, :], ps[0:KC, :]).then_inc(k_hi_ready, 1)
                elif kind == "Q":
                    act.wait_ge(q_done, 2 * b + i + 1)
                    act.copy(q_hi[:, i, :], ps[:, :]).then_inc(q_hi_ready, 1)
                elif kind == "V":
                    act.wait_ge(v_turned, b + 1)
                    act.wait_ge(pv_done, QT * b - QT if not first else 0)
                    act.copy(values[:, par, :, :], ps[:, :].rearrange("p (t d) -> p t d", d=2 * KC)[:, :, KC:])\
                       .then_inc(v_ready, 1)
                elif kind == "M":
                    act.wait_ge(m_turned, b + 1)
                    act.wait_ge(m_loaded, MAX_LOAD * b)
                    act.mul(m_hi[:, :], ps[0:H2, :], -1.0).then_inc(m_hi_ready, 1)
                elif kind == "T":
                    act.wait_ge(oT_turned, 2 * b + i + 1)
                    act.copy(oT[:, i, :], ps[:, :]).then_inc(oT_copied, 1)
                elif kind == "W":
                    act.wait_ge(x2_ready, 2 * b + i + 1)
                    for t in range(2 * i, 2 * i + 2):
                        if t > 0:
                            act.wait_ge(sq_done, QT * b + t)
                        act.activation(squares[:, :], x2[:, t, :], ACT.Square, accum_out=sq_sum[:, t:t + 1]).then_inc(sq_done, 1)
                elif kind == "Y":
                    act.wait_ge(moe_turned, 2 * b + i + 1)
                    act.wait_ge(moe_stored, 16 * b)
                    act.wait_ge(logits_done, b)
                    act.mul(moeT[:, i, :], ps[:, :], g2_sb[:, i:i + 1]).then_inc(moe_ready, 1)
                    if i == 1:
                        act.wait_ge(moe_ready, 2 * b + 2)
                        act.dma_start(x_moe[bass.ds(b, 1)].rearrange("o p h t -> p (o h) t"), moeT[:, :, :])\
                           .then_inc(moe_stored, 16)

                elif kind == "L":
                    act.wait_ge(logits_done, b + 1)
                    act.wait_ge(logits_stored, 16 * b)
                    act.copy(logits_sb[:, :], ps[:, 0:QT * E]).then_inc(logits_copied, 1)
                    act.wait_ge(logits_copied, b + 1)
                    act.dma_start(logits[:, bass.ds(b * (QT * E), QT * E)], logits_sb[:, :]).then_inc(logits_stored, 16)

            def copy_o(b, first=False):
                act.wait_ge(pv_done, QT * b + QT)
                if not first:
                    act.wait_ge(o_turned, QT * b)
                for i in range(2):
                    act.copy(o_pair[:, i, :], ps_o[:, i, :]).then_inc(o_copied, 1)
                act.copy(sums[:, :], ps_r[:, :]).then_inc(o_copied, 1)

            def par_of(kind, par):
                return (par + AHEAD[kind]) % 2

            def body(b, par, lo, hi):
                for k in range(4):
                    for j in range(H2):
                        i = 4 * k + j
                        act.wait_ge(st_ready, 16 * b + i + 1)
                        if lo < 0 or i >= 8:
                            act.wait_ge(pv_done, QT * b + k - 1)
                        act.activation(probs[:, i % 8, :], ps_t[:, i % 2, :], ACT.Exp, scale=KC ** -0.5).then_inc(exp_done, 1)
                        if (k, j) == (0, 3) and lo < 0:
                            copy_o(b - 1)
                        for kind, n, bb in tasks(b, (k, j), lo, hi):
                            task(kind, n, bb, par_of(kind, par))

            for slab, row in ((k_b0, 0), (k_b1, 1)):
                act.copy(slab[:, :, :], key_init[:, row:row + 1, :].broadcast_to([P, 2, T])).then_inc(set_up, 1)
            for kind, i, b in PROLOGUE:
                task(kind, i, b, b % 2, b == 0)
            task("M", 0, 0)
            all_bodies(act, body)
            copy_o(B - 1)
            for kind, i, b in EPILOGUE:
                task(kind, i, b)

        @block.vector
        def _(dve):
            def statistics(b):
                dve.wait_ge(x_loaded, 16 * b + 16)
                for t in range(QT):
                    dve.bn_stats(stats[:, t, :], xt[:, t, :]).then_inc(stat_done, 1)
                dve.wait_ge(stat_done, QT * b + QT)
                dve.tensor_copy(veps_tick[:, 0:1], stats[:, 0, 0:1])
                for t in range(QT):
                    dve.bn_aggr(mv[:, t, :], stats[:, t, :]).then_inc(mv_done, 1)

            def normalize(b):
                dve.wait_ge(r_step, 7 * b + 7)
                dve.wait_ge(xT_turned, 2 * b)
                for t in range(QT):
                    dve.tensor_scalar(xn[:, t, :], xt[:, t, :], mv[:, t, 0:1], r_small[:, 5, t:t + 1],
                                      ALU.subtract, ALU.mult).then_inc(xn_ready, 1)

            def normalize_moe(b):
                dve.wait_ge(rms_step, 2 * b + 2)
                dve.wait_ge(moe_turned, 2 * b)
                dve.wait_ge(tok_stored, 16 * b)
                for t in range(QT):
                    dve.tensor_scalar(xn2[:, t, :], x2[:, t, :], rms2[:, 1, t:t + 1], None, ALU.mult).then_inc(xn2_ready, 1)

            def task(kind, i, b):
                ps = bank(kind, i)
                if kind == "K":
                    dve.wait_ge(k_hi_ready, b + 1)
                    dve.tensor_tensor(k_lo[:, :], ps[0:KC, :], k_hi[:, :].bitcast(F32), ALU.subtract).then_inc(k_lo_ready, 1)
                elif kind == "Q":
                    dve.wait_ge(q_hi_ready, 2 * b + i + 1)
                    dve.tensor_tensor(q_lo[:, i, :], ps[:, :], q_hi[:, i, :].bitcast(F32), ALU.subtract).then_inc(q_lo_ready, 1)
                elif kind == "M":
                    dve.wait_ge(m_hi_ready, b + 1)
                    dve.scalar_tensor_tensor(out=m_lo[:, :], in0=ps[0:H2, :], scalar=-1.0, in1=m_hi[:, :].bitcast(F32),
                                             op0=ALU.mult, op1=ALU.subtract).then_inc(m_lo_ready, 1)
                elif kind == "O":
                    dve.wait_ge(o_turned, QT * b + i + 1)
                    dve.reciprocal(r_sum[:, i, :], ps[:, 2 * P:3 * P].rearrange("p (h e) -> p h e", e=32)[:, :, 0])\
                       .then_inc(r_done, 1)
                    dve.wait_ge(r_done, QT * b + i + 1)
                    dve.tensor_tensor(o_tok[:, i, :].rearrange("p (h d) -> p h d", d=KC),
                                      ps[:, 0:2 * P].rearrange("p (h d) -> p h d", d=KC),
                                      r_sum[:, i, :].unsqueeze(2).broadcast_to([P, H2, KC]), ALU.mult).then_inc(o_normed, 1)
                elif kind == "W":
                    s = slice(2 * i, 2 * i + 2)
                    dve.wait_ge(out_done, 2 * b + i + 1)
                    dve.wait_ge(res_loaded, 32 * b + 32)
                    dve.wait_ge(xn2_ready, QT * b)
                    dve.tensor_tensor(x2[:, s, :].rearrange("p t d -> p (t d)"), ps[:, :],
                                      xf_res[:, s, :].rearrange("p t d -> p (t d)"), ALU.add).then_inc(x2_ready, 1)
                    if i == 1:
                        dve.wait_ge(x2_ready, 2 * b + 2)
                        dve.wait_ge(base_stored, 16 * b)
                        dve.scalar_tensor_tensor(out=base_sb[:, :, :].rearrange("p t d -> p (t d)"),
                                                 in0=x2[:, :, :].rearrange("p t d -> p (t d)"), scalar=gate[:, 0:1],
                                                 in1=x1_res[:, :, :].rearrange("p t d -> p (t d)"),
                                                 op0=ALU.mult, op1=ALU.add).then_inc(base_ready, 1)

            def row_maximum(b, n, t):
                i, h = 4 * n + t, HEAD_ORDER[n]
                dve.wait_ge(s_ready, 16 * b + i + 1)
                if i == 0:
                    dve.wait_ge(m_turned, b)
                dve.tensor_reduce(row_max[:, t, h:h + 1], ps_s[:, i % 2, :], AX.X, ALU.max).then_inc(max_done, 1)

            def body(b, par, lo, hi):
                for k in range(4):
                    for j in range(H2):
                        if (k, j) == (0, 1) and lo <= -2:
                            normalize_moe(b - 2)
                        if (k, j) == (0, 2) and hi >= 2:
                            statistics(b + 2)
                        if (k, j) == (1, 3) and hi >= 2:
                            normalize(b + 2)
                        if k in (1, 2) and hi >= 1:
                            for t in range(2):
                                row_maximum(b + 1, 2 * k - 2 + j // 2, 2 * (j % 2) + t)
                        for t in tasks(b, (k, j), lo, hi):
                            task(*t)

            statistics(0)
            normalize(0)
            dve.wait_ge(consts, 16 * 9)
            zeros = key_init[:, 0:1, :]
            dve.tensor_copy(q_b[:, :, :, :].rearrange("p a h t -> p (a h) t"), zeros.broadcast_to([P, 2 * H2, T])).then_inc(set_up, 1)
            dve.wait_ge(gate_ready, 1)
            for n, (kind, i, b) in enumerate(PROLOGUE):
                if n == 5:
                    statistics(1)
                    normalize(1)
                task(kind, i, b)
            for h in range(H2):
                for t in range(QT):
                    row_maximum(0, h, t)
            task("M", 0, 0)
            all_bodies(dve, body)
            normalize_moe(B - 2)
            for t in EPILOGUE:
                if t == ("Y", 0, B - 1):
                    normalize_moe(B - 1)
                task(*t)

        @block.tensor
        def _(pe):
            pe.wait_ge(consts, 16 * 9)
            last_task = {0: None, 1: None, None: None}

            def task(kind, i, b):
                ps = bank(kind, i)
                if kind == "X":
                    if i == 0:
                        pe.wait_ge(xn_ready, QT * b + QT)
                    for t in range(QT):
                        mm = pe.transpose(ps[:, t * P:(t + 1) * P], xn[:, t, i * P:(i + 1) * P], ident[:, :])
                    mm.then_inc(xT_turned, 1)
                elif kind == "K":
                    pe.wait_ge(xT_copied, 2 * b + 2)
                    for h in range(DH):
                        mm = pe.matmul(ps[:, :], wkv_sb[:, h, :], xnT[:, h, :], start=(h == 0), stop=(h == DH - 1))
                    mm.then_inc(kv_done, 1)
                elif kind == "Q":
                    for h in range(DH):
                        mm = pe.matmul(ps[:, :], wq_sb[:, h, i * P:(i + 1) * P], xnT[:, h, :],
                                       start=(h == 0), stop=(h == DH - 1))
                    mm.then_inc(q_done, 1)
                elif kind == "V":
                    pe.wait_ge(vT_ready, b + 1)
                    for t in range(QT):
                        mm = pe.transpose(ps[:, t * P:(t + 1) * P], vT[:, t * P:(t + 1) * P], ident[:, :])
                    mm.then_inc(v_turned, 1)
                elif kind == "M":
                    pe.wait_ge(max_done, 16 * b + 16)
                    for t in range(QT):
                        mm = pe.transpose(ps[0:H2, t * P:(t + 1) * P], row_max[:, t, :], ident[:, :])
                    mm.then_inc(m_turned, 1)
                elif kind == "O":
                    pe.wait_ge(o_copied, 3 * b + 3)
                    for n, src in enumerate((o_pair[:, 0, :], o_pair[:, 1, :], sums[:, :])):
                        mm = pe.transpose(ps[:, n * P:(n + 1) * P], src[:, i * P:(i + 1) * P], ident[:, :])
                    mm.then_inc(o_turned, 1)
                elif kind == "T":
                    if i == 0:
                        pe.wait_ge(o_normed, QT * b + QT)
                    for t in range(QT):
                        mm = pe.transpose(ps[:, t * P:(t + 1) * P], o_tok[:, t, i * P:(i + 1) * P], ident[:, :])
                    mm.then_inc(oT_turned, 1)
                elif kind == "W":
                    if i == 0:
                        pe.wait_ge(oT_copied, 2 * b + 2)
                    for t in range(2 * i, 2 * i + 2):
                        for h in range(DH):
                            mm = pe.matmul(ps[:, (t % 2) * D:(t % 2 + 1) * D], oT[:, h, t * P:(t + 1) * P],
                                           wo_sb[:, h, :], start=(h == 0), stop=(h == DH - 1))
                    mm.then_inc(out_done, 1)
                elif kind == "Y":
                    pe.wait_ge(xn2_ready, QT * b + QT)
                    for t in range(QT):
                        mm = pe.transpose(ps[:, t * P:(t + 1) * P], xn2[:, t, i * P:(i + 1) * P], ident[:, :])
                    mm.then_inc(moe_turned, 1)
                elif kind == "L":
                    pe.wait_ge(moe_ready, 2 * b + 2)
                    for t in range(QT):
                        for h in range(DH):
                            mm = pe.matmul(ps[:, t * E:(t + 1) * E], moeT[:, h, t * P:(t + 1) * P], wr_sb[:, h, :],
                                           start=(h == 0), stop=(h == DH - 1))
                    mm.then_inc(logits_done, 1)

            def max_scores(b, par, n, t):
                i = 4 * n + t
                if t == 0 and n % 2 == 0:
                    pe.wait_ge(slabs_loaded[par][n // 2], SLAB_LOAD[n // 2] * (b // 2 + 1))
                if i < 2 and last_task[i] is not None:
                    wait_freed(i, b, 1)
                if i >= 2:
                    pe.wait_ge(max_done, 16 * b + i - 1)
                h = HEAD_ORDER[n]
                q = slice(t * P, (t + 1) * P)
                pe.matmul(ps_s[:, i % 2, :], q_a[:, par, h, q], k_a[:, par, :], start=True, stop=False)
                pe.matmul(ps_s[:, i % 2, :], q_b[:, par, h, q], k_b0[:, par, :], start=False, stop=True).then_inc(s_ready, 1)

            def exp_scores(b, par, c, h, first):
                i = 4 * c + h
                if i == 0:
                    pe.wait_ge(m_loaded, MAX_LOAD * (b + 1))
                if not (first and i < 2):
                    pe.wait_ge(exp_done, 16 * b + i - 1)
                k = slice(c * P, (c + 1) * P)
                pe.matmul(ps_t[:, i % 2, :], k_a[:, par, k], q_a[:, par, h, :], start=True, stop=False)
                pe.matmul(ps_t[:, i % 2, :], k_b1[:, par, k], q_b[:, par, h, :], start=False, stop=True).then_inc(st_ready, 1)

            def weigh_values(b, par, c, pair, first):
                pe.wait_ge(exp_done, 16 * b + 4 * c + 2 * pair + 2)
                if c == 0 and pair == 0:
                    pe.wait_ge(v_ready, b + 1)
                    if not first:
                        pe.wait_ge(o_copied, 3 * b)
                for a in range(2):
                    pe.matmul(ps_o[KC * a:KC * a + KC, pair, :], values[:, par, c, :], probs[:, (4 * c + 2 * pair + a) % 8, :],
                              start=(c == 0), stop=(c == QT - 1), skip_group_check=True)

            def sum_probs(b, c):
                for h in range(H2):
                    mm = pe.matmul(ps_r[32 * h:32 * h + 32, :], ones[:, :], probs[:, (4 * c + h) % 8, :],
                                   start=(c == 0), stop=(c == QT - 1), skip_group_check=True)
                mm.then_inc(pv_done, 1)

            def body(b, par, lo, hi):
                first = lo == 0
                for k in range(4):
                    for j in range(H2):
                        if k in (1, 2) and hi >= 1:
                            for t in range(2):
                                max_scores(b + 1, 1 - par, 2 * k - 2 + j // 2, 2 * (j % 2) + t)
                        exp_scores(b, par, k, j, first)
                        if j % 2 == 1 and (k > 0 or not first):
                            bb, pp, c = (b, par, k - 1) if k else (b - 1, 1 - par, 3)
                            weigh_values(bb, pp, c, j // 2, first and k == 1)
                            if j == 3:
                                sum_probs(bb, c)
                        for kind, n, bb in tasks(b, (k, j), lo, hi):
                            run(kind, n, bb, AHEAD[kind])

            def wait_freed(place, b, ahead):
                pk, pn, pahead = last_task[place]
                for s, v in freed(pk, pn, b + (pahead - ahead)):
                    pe.wait_ge(s, v)

            def run(kind, n, b, ahead):
                place = SPARE.get((kind, n))
                if last_task[place] is not None:
                    wait_freed(place, b, ahead)
                if place is not None and (kind, n) != ("Q", 1) and scored[0]:
                    pe.wait_ge(max_done, 16 * (b - ahead + 1) + 16 * (kind in "KQ"))
                task(kind, n, b)
                last_task[place] = (kind, n, ahead)

            scored = [False]
            for kind, i, b in PROLOGUE:
                run(kind, i, b, b)
            for place in (0, 1):
                last_task[place] = last_task[place][:2] + (last_task[place][2] + 1,)
            for h in range(H2):
                for t in range(QT):
                    max_scores(0, 0, h, t)
            scored[0] = True
            run("M", 0, 0, 0)
            for place in (0, 1):
                last_task[place] = None
            body(0, 0, 0, 2)
            def bodies():
                def nxt():
                    for place, t in last_task.items():
                        last_task[place] = (t[0], t[1], t[2] - 1)
                nxt()
                body(1, 1, -1, 2)
                nxt()
                with pe.Fori(2, B - 3, 2) as b:
                    body(b, 0, -2, 2)
                    nxt()
                    body(b + 1, 1, -2, 2)
                    nxt()
                body(B - 2, 0, -2, 1)
                nxt()
                body(B - 1, 1, -2, 0)

            bodies()
            for pair in range(2):
                weigh_values(B - 1, 1, QT - 1, pair, False)
            sum_probs(B - 1, QT - 1)
            for place, t in last_task.items():
                last_task[place] = (t[0], t[1], B - 1 + t[2])
            scored[0] = False
            for kind, i, b in EPILOGUE:
                run(kind, i, b, b)


F = 256
N_W = E + 1
W13 = DH * 2 * F
W_ALL = W13 + F // P * D
N = B * T
TOP = 2
ROW = D + 2
REGION = N + P
DUMP = E * REGION
TILES = -(-((TOP * N + E * (P - 1)) // P) // 8) * 8
MORE = TILES - TOP * N // P
ROWS_X = DUMP + MORE * P
ROWS_Y = TOP * N + (E + MORE) * P
STEPS = N // P
NT = N // P
Y_DEPTH = 4
Y_BUFS = 4
GROUP = 8


def experts(nc, x_moe, x_tok, logits_in, base, g_ffn, g2, bias, w13T, w2T, iota, identity, before, steps, upto,
            tile_ids, place0, dest0, blank, rows_x, rows_y, out):
    with ExitStack() as ctx:
        def sb(name, shape, dt=F32):
            return ctx.enter_context(nc.sbuf_tensor("mo_" + name, shape, dt))

        def psum(name, shape):
            return ctx.enter_context(nc.psum_tensor("mo_" + name, shape, F32))

        def sem(name):
            return ctx.enter_context(nc.semaphore("mo_" + name))

        bias_sb = sb("bias", [P, E])
        gate = sb("gate", [P, 1])
        g2_sb = sb("g2", [P, DH])
        tick = sb("tick", [P, 2])
        zeros = sb("zeros", [P, TOP * QT])
        iota_sb = sb("iota", [P, E])
        ident = sb("ident", [P, P])
        before_sb = sb("before", [P, 2, P])
        steps_sb = sb("steps", [P, STEPS])
        upto_sb = sb("upto", [P, E, E])
        tile_ids_sb = sb("tile_ids", [P, TILES])
        place_base = sb("place_base", [P, E])
        stage = sb("stage", [P, 2, W_ALL])
        w_hi = sb("w_hi", [P, N_W * W_ALL], F32R)
        w_lo = sb("w_lo", [P, N_W * W_ALL], F32R)
        xT = sb("xT", [P, DH, T])
        x_hi = sb("x_hi", [P, DH, T], F32R)
        x_lo = sb("x_lo", [P, DH, T], F32R)
        x_rows = sb("x_rows", [P, 2, TOP, QT, ROW])
        top = sb("top", [P, NT])
        psums = sb("psums", [P, NT])
        where_f = sb("where_f", [P, NT, 2])
        w_top = sb("w_top", [P, 3, NT])
        extras = sb("extras", [P, TOP, NT, 2])
        slot_f = sb("slot_f", [P, TOP, NT])
        slot_u = sb("slot_u", [P, TOP, NT], U32)
        slots = sb("slots", [P, 2, TOP, QT], U32)
        n_expert = sb("n_expert", [P, E])
        n_steps = sb("n_steps", [P, E, STEPS])
        n_tiles = sb("n_tiles", [P, E])
        ends = sb("ends", [P, E, E])
        end = sb("end", [P, E])
        past = sb("past", [P, 2, TILES, E])
        table_f = sb("table_f", [P, 2, TILES])
        expert_table = sb("expert_table", [P, TILES + 2], U32)
        row_table = sb("row_table", [P, TILES], U32)
        blank_f = sb("blank_f", [P, E])
        blank_at = sb("blank_at", [P, E], U32)
        dest_u = sb("dest_u", [P, Y_BUFS], U32)
        s_act = sb("s_act", [P, 2, T])
        h_full = sb("h_full", [P, 2, T])
        h_hi = sb("h_hi", [P, 2, T], F32R)
        h_lo = sb("h_lo", [P, 2, T], F32R)
        acc = sb("acc", [P, B, QT, D])

        LATE = 3
        scratch = acc[:, B - LATE:B, :, :].rearrange("p b t d -> p (b t d)")

        def scratch_of(n, dt=F32):
            ap = scratch[:, n * NT * E:(n + 1) * NT * E].rearrange("p (t e) -> p t e", e=E)
            return ap.bitcast(dt) if dt != F32 else ap

        logits, probs, best, place = (scratch_of(i) for i in range(4))
        where = scratch_of(4, U32)
        chosen, places, scan = [scratch_of(5), scratch_of(6)], [scratch_of(8), scratch_of(9)], [scratch_of(10), scratch_of(11)]
        both = scratch_of(7)

        ps_h = psum("ps_h", [P, 2, 2, T])
        ps_y = psum("ps_y", [P, QT, T])
        ps_n = ps_y[:, QT - 1, :]

        x_tiles = x_rows[:, 0, :, :, :].rearrange("p j t r -> p (j t) r")
        ps_x, ps_t = ps_h[:, 1, 0, 0:D], ps_h[:, 1, 1, 0:D]

        route_consts = sem("route_consts")
        consts = sem("consts")
        gate_ready = sem("gate_ready")
        w_loaded = [sem(f"w_loaded{i}") for i in range(2)]
        hi_ready = sem("w_hi_ready")
        lo_ready = sem("w_lo_ready")
        x_loaded = sem("x_loaded")
        rows_loaded = [sem(f"rows_loaded{i}") for i in range(2)]
        base_loaded = sem("base_loaded")
        xh_ready = sem("xh_ready")
        xl_ready = sem("xl_ready")
        route = sem("route")
        exp_done = sem("exp_done")
        rank_done = sem("rank_done")
        slot_step = sem("slot_step")
        slots_ready = sem("slots_ready")
        scattered = [sem(f"scattered{i}") for i in range(2)]
        table_step = sem("table_step")
        pool_step = sem("pool_step")
        h_done = sem("h_done")
        silu_done = sem("silu_done")
        h_ready = sem("h_ready")
        hh_ready = sem("hh_ready")
        hl_ready = sem("hl_ready")
        y_done = sem("y_done")
        acc_step = sem("acc_step")

        tile_loaded = [sem(f"tile_loaded{i}") for i in range(GROUP)]
        t_x_turned = sem("t_x_turned")
        t_x_hi = sem("t_x_hi")
        t_x_lo = sem("t_x_lo")
        t_h_done = sem("t_h_done")
        t_silu = sem("t_silu")
        t_h = sem("t_h")
        t_h_turned = sem("t_h_turned")
        t_h_hi = sem("t_h_hi")
        t_h_lo = sem("t_h_lo")
        t_y_done = sem("t_y_done")
        t_y = sem("t_y")
        t_scattered = [sem(f"t_scattered{i}") for i in range(Y_BUFS)]
        stored = sem("stored")

        def rows(ap, b):
            return ap.rearrange("b (t p) d -> b p t d", p=P)[bass.ds(b, 1)].rearrange("o p t d -> p (o t) d")

        N_ROUTE_CONST, N_CONST = 7, 6
        CHOSEN = 12
        TABLE = 12
        BATCH_ROWS = 16 * TOP * QT
        stage_flat = stage[:, :, :].rearrange("p a f -> p (a f)")

        def tile_y(u):
            return stage_flat[:, u * D:(u + 1) * D]

        def y_buffer(k, j):
            rows_flat = x_rows[:, :, :, :, :].rearrange("p a j t r -> p (a j t r)")
            at = [stage_flat[:, n * QT * D:] for n in range(3)] + [rows_flat[:, n * QT * D:] for n in range(4)] + \
                 [xT[:, :, :].rearrange("p h t -> p (h t)")]
            return at[TOP * k + j][:, 0:QT * D].rearrange("p (t d) -> p t d", d=D)

        def all_batches(eng, body):
            for k in range(2):
                body(k, k, 0, first=True)
            with eng.Fori(1, B // 2 - 1) as r:
                for k in range(2):
                    body(2 * r + k, k, r)
            for k in range(2):
                body(B - 2 + k, k, B // 2 - 1, last=(k == 1))

        def all_tiles(eng, body, load=None):
            def group(first, r, **how):
                values = load(first) if load else None
                for u in range(GROUP):
                    body(first + u, u, r, values, **how)

            group(0, 0)
            with eng.Fori(1, TILES // GROUP - 1) as r:
                group(GROUP * r, r, inner=True)
            group(TILES - GROUP, TILES // GROUP - 1, inner=True, last=True)

        def from_table(engine, ap, least, most):
            return nc.values_load_multi_w_load_instructions(ap, engines=[engine], min_val=least, max_val=most,
                                                            skip_runtime_bounds_check_because="the tables are clamped")[1]

        block = ctx.enter_context(nc.Block())

        @block.sync
        def _(sp):
            def load(b):
                sp.dma_start(xT[:, :, :], x_moe[bass.ds(b, 1)].rearrange("o p h t -> p (o h) t")).then_inc(x_loaded, 16)

            def load_rows(b, k):
                for j in range(TOP):
                    sp.dma_start(x_rows[:, k, j, :, 0:D], rows(x_tok, b)).then_inc(rows_loaded[k], 16)

            def load_w(e, k):
                for at, src in ((slice(0, W13), w13T), (slice(W13, W_ALL), w2T)):
                    sp.dma_start(stage[:, k, at].rearrange("p (h f) -> p h f", h=2),
                                 src[bass.ds(e, 1)].rearrange("o (h p) f -> p (o h) f", p=P)).then_inc(w_loaded[k], 16)

            sp.dma_start(logits, logits_in.rearrange("p (t e) -> p t e", e=E)).then_inc(route_consts, 16)
            for dst, src in ((bias_sb, bias), (gate, g_ffn), (iota_sb, iota), (place_base, place0)):
                sp.dma_start(dst[:, :], src.partition_broadcast(P)).then_inc(route_consts, 16)
            sp.dma_start(before_sb[:, :, :], before).then_inc(route_consts, 16)
            sp.dma_start(extras[:, :, :, :], dest0).then_inc(route_consts, 16)
            load(0)
            load_w(0, 0)
            for dst, src in ((steps_sb, steps), (tile_ids_sb, tile_ids)):
                sp.dma_start(dst[:, :], src.partition_broadcast(P)).then_inc(consts, 16)
            for dst, src in ((g2_sb, g2), (ident, identity)):
                sp.dma_start(dst[:, :], src).then_inc(consts, 16)
            sp.dma_start(upto_sb[:, :, :].rearrange("p a b -> p (a b)"), upto.partition_broadcast(P)).then_inc(consts, 16)
            sp.dma_start(rows_x[DUMP:ROWS_X, :].rearrange("(m p) r -> p m r", p=P), blank[:, E:E + MORE, :]).then_inc(consts, 16)
            load_w(1, 1)
            for k in range(2):
                load_rows(k, k)

            def load_base(first, past):
                sp.dma_start(acc[:, first:past, :, :].rearrange("p b t d -> p (b t) d"),
                             base[first:past].rearrange("b (t p) d -> p (b t) d", p=P)).then_inc(base_loaded, 16)

            load_base(0, B - LATE)

            def batch(b, k, r, first=False, last=False):
                if not first:
                    sp.wait_ge(scattered[k], BATCH_ROWS * r)
                    load_rows(b, k)
                if not last:
                    sp.wait_ge(xl_ready, b + 1)
                    load(b + 1)
                if not last:
                    sp.wait_ge(hi_ready, b + 1)
                    sp.wait_ge(lo_ready, b + 1)
                    load_w(b + 2, k)
                if first and k == 1:
                    sp.wait_ge(slots_ready, 1)
                    load_base(B - LATE, B)

            all_batches(sp, batch)
            sp.wait_ge(table_step, TABLE)
            behind = from_table(mybir.EngineType.SP, blank_at[0:1, :], 0, DUMP - P)
            for e in range(E):
                sp.dma_start(rows_x[bass.ds(behind[e], P), :], blank[:, e, :]).then_inc(consts, 16)

            for k in range(2):
                sp.wait_ge(scattered[k], BATCH_ROWS * B // 2)
            sp.wait_ge(consts, 16 * (N_CONST + E))

            def load_tile(i, u, r, values, inner=False, last=False):
                if inner:
                    sp.wait_ge(t_y, i - GROUP + 1)
                sp.dma_start(x_tiles[:, u, :], rows_x[bass.ds(values[u], P), :]).then_inc(tile_loaded[u], 16)

            all_tiles(sp, load_tile, lambda i: from_table(mybir.EngineType.SP, row_table[0:1, bass.ds(i, GROUP)], 0, ROWS_X - P))

            for n in range(Y_BUFS):
                sp.wait_ge(t_scattered[n], 16 * (TILES // Y_BUFS))
            y_v = rows_y[0:TOP * N, :].rearrange("(j b t p) d -> b j p t d", p=P, t=QT, b=B)

            def load_y(b):
                for j in range(TOP):
                    sp.dma_start(y_buffer(b % Y_DEPTH, j), y_v[b, j]).then_inc(tile_loaded[b % Y_DEPTH], 16)

            for b in range(Y_DEPTH):
                load_y(b)
            for b in range(B):
                sp.wait_ge(acc_step, QT * B + 2 * b + 2)
                if b + Y_DEPTH < B:
                    load_y(b + Y_DEPTH)
                sp.dma_start(rows(out, b), acc[:, b, :, :]).then_inc(stored, 16)
            sp.wait_ge(stored, 16 * B)

        @block.gpsimd
        def _(pool):
            pool.memset(zeros[:, :], 0.0)
            pool.memset(tick[:, :], 0.0).then_inc(gate_ready, 1)
            pool.wait_ge(route_consts, 16 * N_ROUTE_CONST)
            pool.wait_ge(gate_ready, 2)

            def bear_wait():
                pool.tensor_tensor(tick[:, 1:2], tick[:, 0:1], tick[:, 0:1], ALU.add).then_inc(pool_step, 1)

            def scatter(dst, index, src, signal):
                pool.indirect_dma_start(dst, bass.IndirectOffsetOnAxis(ap=index, axis=0), src, None).then_inc(signal, 16)

            def batch(b, k, r, first=False, last=False):
                pool.wait_ge(rows_loaded[k], 32 * r + 32)
                if not first:
                    pool.wait_ge(scattered[k], BATCH_ROWS * r)
                if not (first and k == 0):
                    pool.wait_ge(pool_step, 3 * b)
                bear_wait()
                for j in range(TOP):
                    pool.tensor_tensor(x_rows[:, k, j, :, D:ROW], extras[:, j, bass.ds(QT * b, QT), :],
                                       zeros[:, 0:2 * QT].rearrange("p (t w) -> p t w", w=2), ALU.add)
                pool.tensor_tensor(slots[:, k, :, :], slot_u[:, :, bass.ds(QT * b, QT)],
                                   zeros[:, :].bitcast(U32).rearrange("p (j t) -> p j t", t=QT), ALU.add).then_inc(pool_step, 1)
                pool.wait_ge(pool_step, 3 * b + 2)
                bear_wait()
                for t in range(QT):
                    for j in range(TOP):
                        scatter(rows_x, slots[:, k, j, t:t + 1], x_rows[:, k, j, t, :], scattered[k])

            pool.wait_ge(slots_ready, 1)
            all_batches(pool, batch)
            def scatter_tile(i, u, r, values, inner=False, last=False):
                pool.wait_ge(pool_step, 3 * B + i)
                pool.wait_ge(t_y, i + 1)
                bear_wait()
                n = u % Y_BUFS
                scatter(rows_y, dest_u[:, n:n + 1], tile_y(n), t_scattered[n])

            all_tiles(pool, scatter_tile)

        @block.scalar
        def _(act):

            def split_w(e, k, r):
                act.wait_ge(w_loaded[k], 32 * r + 32)
                act.copy(w_hi[:, bass.ds(e * W_ALL, W_ALL)], stage[:, k, :]).then_inc(hi_ready, 1)

            def split_x(b):
                act.wait_ge(x_loaded, 16 * b + 16)
                act.wait_ge(h_done, 2 * b)
                act.copy(x_hi[:, :, :], xT[:, :, :]).then_inc(xh_ready, 1)

            act.wait_ge(route_consts, 16 * N_ROUTE_CONST)
            act.activation(gate[:, :], gate[:, :], ACT.Tanh).then_inc(gate_ready, 1)
            act.wait_ge(route, 3)
            act.activation(probs, logits, ACT.Exp).then_inc(exp_done, 1)
            split_x(0)
            split_w(0, 0, 0)
            act.wait_ge(route, 8)
            act.activation(w_top[:, 1, :], w_top[:, 0, :], ACT.Exp).then_inc(exp_done, 1)

            def batch(b, k, r, first=False, last=False):
                for u in range(2):
                    act.wait_ge(h_done, 2 * b + u + 1)
                    act.wait_ge(h_ready, 2 * b)
                    act.activation(s_act[:, u, :], ps_h[:, u, 0, :], ACT.Silu).then_inc(silu_done, 1)
                    act.wait_ge(h_ready, 2 * b + u + 1)
                    act.wait_ge(y_done, QT * b)
                    act.copy(h_hi[:, u, :], h_full[:, u, :]).then_inc(hh_ready, 1)
                if not last:
                    split_x(b + 1)
                split_w(b + 1, 1 - k, r + k)

            all_batches(act, batch)
            act.wait_ge(consts, 16 * N_CONST)

            def x_high(i, par):
                act.wait_ge(t_x_turned, i + 1)
                for h in range(DH):
                    ins = act.mul(x_hi[:, par, h * P:(h + 1) * P], ps_x[:, h * P:(h + 1) * P], g2_sb[:, h:h + 1])
                ins.then_inc(t_x_hi, 1)

            def h_high(i, par, again):
                act.wait_ge(t_h_turned, i + 1)
                if again:
                    act.wait_ge(t_y_done, i - 1)
                act.copy(h_hi[:, par, 0:F], ps_t).then_inc(t_h_hi, 1)

            def body(i, u, r, values, inner=False, last=False):
                act.wait_ge(t_h_done, i + 1)
                if inner or u >= 2:
                    act.wait_ge(t_h, i - 1)
                act.activation(s_act[:, u % 2, 0:F], ps_h[:, 0, u % 2, 0:F], ACT.Silu).then_inc(t_silu, 1)
                if inner or u >= 1:
                    h_high(i - 1, (u - 1) % 2, inner or u >= 3)
                if not (last and u >= GROUP - 2):
                    x_high(i + 2, u % 2)

            x_high(0, 0)
            x_high(1, 1)
            all_tiles(act, body)
            h_high(TILES - 1, 1, True)

        @block.vector
        def _(dve):
            def split_w(e, k):
                dve.wait_ge(hi_ready, e + 1)
                at = bass.ds(e * W_ALL, W_ALL)
                dve.tensor_tensor(w_lo[:, at], stage[:, k, :], w_hi[:, at].bitcast(F32), ALU.subtract).then_inc(lo_ready, 1)

            def split_x(b):
                dve.wait_ge(xh_ready, b + 1)
                dve.tensor_tensor(x_lo[:, :, :], xT[:, :, :], x_hi[:, :, :].bitcast(F32), ALU.subtract).then_inc(xl_ready, 1)

            def tables():
                m = [1]

                def entry(ins):
                    m[0] += 1
                    ins.then_inc(table_step, 1)
                    dve.wait_ge(table_step, m[0])

                dve.wait_ge(consts, 16 * N_CONST)
                dve.wait_ge(table_step, 1)
                dve.tensor_tensor(blank_f[:, :], place_base[:, :], n_expert[:, :], ALU.add)
                entry(dve.tensor_tensor(n_steps[:, :, :], n_expert[:, :].unsqueeze(2).broadcast_to([P, E, STEPS]),
                                        steps_sb[:, :].unsqueeze(1).broadcast_to([P, E, STEPS]), ALU.is_gt))
                dve.tensor_copy(blank_at[:, :], blank_f[:, :])
                entry(dve.tensor_reduce(n_tiles[:, :], n_steps[:, :, :], AX.X, ALU.add))
                entry(dve.tensor_tensor(ends[:, :, :], n_tiles[:, :].unsqueeze(1).broadcast_to([P, E, E]), upto_sb[:, :, :], ALU.mult))
                entry(dve.tensor_reduce(end[:, :], ends[:, :, :], AX.X, ALU.add))
                entry(dve.tensor_tensor(past[:, 0, :, :], tile_ids_sb[:, :].unsqueeze(2).broadcast_to([P, TILES, E]),
                                        end[:, :].unsqueeze(1).broadcast_to([P, TILES, E]), ALU.is_ge))
                dve.tensor_reduce(table_f[:, 0, :], past[:, 0, :, :], AX.X, ALU.add)
                entry(dve.tensor_scalar(n_tiles[:, :], n_tiles[:, :], -float(P), float(REGION), ALU.mult, ALU.add))
                entry(dve.tensor_scalar(table_f[:, 0, :], table_f[:, 0, :], 1.0, float(E), ALU.add, ALU.min))
                entry(dve.tensor_scalar(table_f[:, 0, :], table_f[:, 0, :], float(W_ALL), None, ALU.mult))
                entry(dve.tensor_tensor(past[:, 1, :, :], past[:, 0, :, :], n_tiles[:, :].unsqueeze(1).broadcast_to([P, TILES, E]), ALU.mult))
                dve.tensor_copy(expert_table[:, 2:TILES + 2], table_f[:, 0, :])
                dve.tensor_copy(expert_table[:, 0:2], table_f[:, 0, 0:2])
                entry(dve.tensor_reduce(table_f[:, 1, :], past[:, 1, :, :], AX.X, ALU.add))
                entry(dve.scalar_tensor_tensor(out=row_table[:, :], in0=tile_ids_sb[:, :], scalar=float(P), in1=table_f[:, 1, :],
                                               op0=ALU.mult, op1=ALU.add))

            dve.wait_ge(route_consts, 16 * N_ROUTE_CONST)
            dve.wait_ge(gate_ready, 2)

            step = [0]

            def chain(ins):
                step[0] += 1
                ins.then_inc(route, 1)
                dve.wait_ge(route, step[0])

            def over_tokens(ap):
                return ap.unsqueeze(1).broadcast_to([P, NT, E])

            def over_experts(ap):
                return ap.unsqueeze(2).broadcast_to([P, NT, E])

            chain(dve.tensor_tensor(logits, logits, over_tokens(bias_sb[:, :]), ALU.add))
            chain(dve.tensor_reduce(top[:, :], logits, AX.X, ALU.max))
            chain(dve.tensor_tensor(logits, logits, over_experts(top[:, :]), ALU.subtract))
            dve.wait_ge(exp_done, 1)
            chain(dve.tensor_reduce(psums[:, :], probs, AX.X, ALU.add))
            chain(dve.reciprocal(psums[:, :], psums[:, :]))
            chain(dve.tensor_tensor(probs, probs, over_experts(psums[:, :]), ALU.mult))
            for t in range(NT):
                ins = dve.max(best[:, t, :], probs[:, t, :])
            chain(ins)
            chain(dve.tensor_tensor(w_top[:, 0, :], best[:, :, 1], best[:, :, 0], ALU.subtract))
            for t in range(NT):
                ins = dve.max_index(where[:, t, :], best[:, t, :], probs[:, t, :])
            chain(ins)
            chain(dve.tensor_copy(where_f[:, :, :], where[:, :, 0:2]))
            for j in range(TOP):
                ins = dve.tensor_tensor(chosen[j], over_tokens(iota_sb[:, :]), over_experts(where_f[:, :, j]), ALU.is_equal)
            chain(ins)
            chain(dve.tensor_tensor(both, chosen[0], chosen[1], ALU.add))
            split_x(0)
            split_w(0, 0)
            dve.wait_ge(exp_done, 2)
            chain(dve.tensor_scalar(w_top[:, 2, :], w_top[:, 1, :], 1.0, None, ALU.add))
            chain(dve.reciprocal(w_top[:, 2, :], w_top[:, 2, :]))
            chain(dve.tensor_scalar(extras[:, 0, :, 0], w_top[:, 2, :], gate[:, 0:1], None, ALU.mult))
            chain(dve.tensor_tensor(extras[:, 1, :, 0], w_top[:, 1, :], extras[:, 0, :, 0], ALU.mult))

            dve.wait_ge(rank_done, 1)
            ranks = ps_n[:, 0:NT * E].rearrange("p (t e) -> p t e", e=E)
            totals = ps_n[:, NT * E:2 * NT * E].rearrange("p (t e) -> p t e", e=E)
            chain(dve.tensor_copy(scan[0], totals))
            n, far = 0, 1
            while far < NT:
                dve.tensor_copy(scan[1 - n][:, 0:far, :], scan[n][:, 0:far, :])
                chain(dve.tensor_tensor(scan[1 - n][:, far:NT, :], scan[n][:, far:NT, :], scan[n][:, 0:NT - far, :], ALU.add))
                n, far = 1 - n, 2 * far
            dve.tensor_copy(n_expert[:, :], scan[n][:, NT - 1, :]).then_inc(table_step, 1)
            chain(dve.tensor_tensor(scan[1 - n], scan[n], totals, ALU.subtract))
            chain(dve.tensor_tensor(place, ranks, scan[1 - n], ALU.add))
            chain(dve.tensor_tensor(place, place, over_tokens(place_base[:, :]), ALU.add))
            for j in range(TOP):
                ins = dve.tensor_tensor(places[j], place, chosen[j], ALU.mult)
            chain(ins)
            for j in range(TOP):
                ins = dve.tensor_reduce(slot_f[:, j, :], places[j], AX.X, ALU.add)
            chain(ins)
            dve.tensor_copy(slot_u[:, :, :], slot_f[:, :, :]).then_inc(slots_ready, 1)

            def batch(b, k, r, first=False, last=False):
                for u in range(2):
                    dve.wait_ge(silu_done, 2 * b + u + 1)
                    dve.wait_ge(hh_ready, 2 * b)
                    dve.tensor_tensor(h_full[:, u, :], s_act[:, u, :], ps_h[:, u, 1, :], ALU.mult).then_inc(h_ready, 1)
                    dve.wait_ge(hh_ready, 2 * b + u + 1)
                    dve.tensor_tensor(h_lo[:, u, :], h_full[:, u, :], h_hi[:, u, :].bitcast(F32), ALU.subtract).then_inc(hl_ready, 1)
                if not last:
                    split_x(b + 1)
                dve.wait_ge(base_loaded, 16 if first else 32)
                for t in range(QT):
                    dve.wait_ge(y_done, QT * b + t + 1)
                    here = acc[:, bass.ds(b, 1), t, :].rearrange("p o d -> p (o d)")
                    dve.scalar_tensor_tensor(out=here, in0=ps_y[:, t, 0:D], scalar=gate[:, 0:1],
                                             in1=here, op0=ALU.mult, op1=ALU.add).then_inc(acc_step, 1)
                split_w(b + 1, 1 - k)

            for k in range(2):
                batch(k, k, 0, first=True)
            tables()
            with dve.Fori(1, B // 2 - 1) as r:
                for k in range(2):
                    batch(2 * r + k, k, r)
            for k in range(2):
                batch(B - 2 + k, k, B // 2 - 1, last=(k == 1))

            def x_low(i, par):
                dve.wait_ge(t_x_hi, i + 1)
                for h in range(DH):
                    c = slice(h * P, (h + 1) * P)
                    ins = dve.scalar_tensor_tensor(out=x_lo[:, par, c], in0=ps_x[:, c], scalar=g2_sb[:, h:h + 1],
                                                   in1=x_hi[:, par, c].bitcast(F32), op0=ALU.mult, op1=ALU.subtract)
                ins.then_inc(t_x_lo, 1)

            def h_low(i, par):
                dve.wait_ge(t_h_hi, i + 1)
                dve.tensor_tensor(h_lo[:, par, 0:F], ps_t, h_hi[:, par, 0:F].bitcast(F32), ALU.subtract).then_inc(t_h_lo, 1)

            def weigh(i, u, r, inner):
                dve.wait_ge(t_y_done, i + 1)
                n = u % Y_BUFS
                if inner or u >= Y_BUFS:
                    dve.wait_ge(t_scattered[n], 16 * (GROUP // Y_BUFS) * r + 16 * (u // Y_BUFS))
                dve.tensor_copy(dest_u[:, n:n + 1], x_tiles[:, u, D + 1:D + 2])
                dve.tensor_scalar(tile_y(n), ps_y[:, u % QT, 0:D], x_tiles[:, u, D:D + 1], None, ALU.mult).then_inc(t_y, 1)

            def body(i, u, r, values, inner=False, last=False):
                dve.wait_ge(t_silu, i + 1)
                if inner or u >= 2:
                    dve.wait_ge(t_h_turned, i - 1)
                dve.tensor_tensor(h_full[:, u % 2, 0:F], s_act[:, u % 2, 0:F], ps_h[:, 0, u % 2, F:2 * F], ALU.mult).then_inc(t_h, 1)
                if inner or u >= 1:
                    h_low(i - 1, (u - 1) % 2)
                if not (last and u >= GROUP - 2):
                    x_low(i + 2, u % 2)
                if u >= 2:
                    weigh(i - 2, u - 2, r, inner)
                elif inner:
                    weigh(i - 2, GROUP + u - 2, r - 1, True)

            x_low(0, 0)
            x_low(1, 1)
            all_tiles(dve, body)
            h_low(TILES - 1, 1)
            for u in (GROUP - 2, GROUP - 1):
                weigh(TILES - GROUP + u, u, TILES // GROUP - 1, True)

            for b in range(B):
                dve.wait_ge(tile_loaded[b % Y_DEPTH], 16 * (TILES // GROUP) + 32 * (b // Y_DEPTH + 1))
                dve.tensor_tensor(acc[:, b, :, :], acc[:, b, :, :], y_buffer(b % Y_DEPTH, 0), ALU.add).then_inc(acc_step, 1)
                dve.wait_ge(acc_step, QT * B + 2 * b + 1)
                dve.tensor_tensor(acc[:, b, :, :], acc[:, b, :, :], y_buffer(b % Y_DEPTH, 1), ALU.add).then_inc(acc_step, 1)

        @block.tensor
        def _(pe):
            pe.wait_ge(route_consts, 16 * N_ROUTE_CONST)
            pe.wait_ge(route, CHOSEN)
            for n in range(2):
                mm = pe.matmul(ps_n[:, n * NT * E:(n + 1) * NT * E], before_sb[:, n, :],
                               both.rearrange("p t e -> p (t e)"), start=True, stop=True)
            mm.then_inc(rank_done, 1)

            def batch(b, k, r, first=False, last=False):
                pe.wait_ge(xl_ready, b + 1)
                pe.wait_ge(lo_ready, 1)
                for f in range(2):
                    pe.wait_ge(h_ready, 2 * b)
                    for g in range(2):
                        n = 0
                        for h in range(DH):
                            for w, x in ((w_hi, x_hi), (w_hi, x_lo), (w_lo, x_hi)):
                                mm = pe.matmul(ps_h[:, f, g, :], w[:, (2 * h + g) * F + f * P:(2 * h + g) * F + (f + 1) * P], x[:, h, :],
                                               start=(n == 0), stop=(n == 5))
                                n += 1
                    mm.then_inc(h_done, 1)
                if first and k == 0:
                    pe.wait_ge(slots_ready, 1)
                pe.wait_ge(acc_step, QT * b)
                for h in range(2):
                    pe.wait_ge(hl_ready, 2 * b + h + 1)
                    for t in range(QT):
                        for n, (hh, w) in enumerate(((h_hi, w_hi), (h_hi, w_lo), (h_lo, w_hi))):
                            mm = pe.matmul(ps_y[:, t, 0:D], hh[:, h, t * P:(t + 1) * P], w[:, W13 + h * D:W13 + (h + 1) * D],
                                           start=(h == 0 and n == 0), stop=(h == 1 and n == 2))
                        if h == 1:
                            mm.then_inc(y_done, 1)

            all_batches(pe, batch)

            pe.wait_ge(table_step, TABLE)
            pe.wait_ge(consts, 16 * N_CONST)
            pe.wait_ge(lo_ready, N_W)
            pe.wait_ge(acc_step, QT * B)
            pe.wait_ge(h_ready, 2 * B)

            def turn_x(i, u, r, again):
                pe.wait_ge(tile_loaded[u], 16 * r + 16)
                if again:
                    pe.wait_ge(t_x_lo, i)
                for h in range(DH):
                    mm = pe.transpose(ps_x[:, h * P:(h + 1) * P], x_tiles[:, u, h * P:(h + 1) * P], ident[:, :])
                mm.then_inc(t_x_turned, 1)

            def turn_h(i, par, again):
                pe.wait_ge(t_h, i + 1)
                if again:
                    pe.wait_ge(t_h_lo, i)
                for h in range(DH):
                    mm = pe.transpose(ps_t[:, h * P:(h + 1) * P], h_full[:, par, h * P:(h + 1) * P], ident[:, :])
                mm.then_inc(t_h_turned, 1)

            def second(i, u, w_at, again):
                if again:
                    pe.wait_ge(t_y, i - QT + 1)
                pe.wait_ge(t_h_lo, i + 1)
                n = 0
                for h in range(2):
                    for hh, w in ((h_hi, w_hi), (h_hi, w_lo), (h_lo, w_hi)):
                        mm = pe.matmul(ps_y[:, u % QT, 0:D], hh[:, u % 2, h * P:(h + 1) * P],
                                       w[:, bass.ds(w_at + (W13 + h * D), D)], start=(n == 0), stop=(n == 5))
                        n += 1
                mm.then_inc(t_y_done, 1)

            def body(i, u, r, values, inner=False, last=False):
                if inner or u >= 2:
                    pe.wait_ge(t_h, i - 1)
                pe.wait_ge(t_x_lo, i + 1)
                n = 0
                for h in range(DH):
                    for w, x in ((w_hi, x_hi), (w_hi, x_lo), (w_lo, x_hi)):
                        mm = pe.matmul(ps_h[:, 0, u % 2, :], x[:, u % 2, h * P:(h + 1) * P],
                                       w[:, bass.ds(values[u + 2] + h * 2 * F, 2 * F)], start=(n == 0), stop=(n == 5))
                        n += 1
                mm.then_inc(t_h_done, 1)
                if inner or u >= 1:
                    turn_h(i - 1, (u - 1) % 2, inner or u >= 2)
                if not (last and u >= GROUP - 2):
                    turn_x(i + 2, (u + 2) % GROUP, r + (u + 2) // GROUP, True)
                if inner or u >= 2:
                    second(i - 2, (u - 2) % GROUP, values[u], inner or u >= QT + 2)
                if last and u == GROUP - 1:
                    turn_h(i, u % 2, True)
                    second(i - 1, u - 1, values[u + 1], True)
                    second(i, u, values[u + 2], True)

            turn_x(0, 0, 0, False)
            turn_x(1, 1, 0, True)

            def experts_of(i):
                return from_table(mybir.EngineType.PE, expert_table[0:1, bass.ds(i, GROUP + 2)], W_ALL, E * W_ALL)

            all_tiles(pe, body, experts_of)


def routing_constants():
    import numpy as np
    f = np.float32
    blank = np.zeros((P, E + MORE, ROW), f)
    blank[:, :, D + 1] = TOP * N + np.arange(P)[:, None] + P * np.arange(E + MORE)
    dest0 = np.zeros((P, TOP, NT, 2), f)
    dest0[:, :, :, 1] = np.arange(P)[:, None, None] + N * np.arange(TOP)[:, None] + P * np.arange(NT)
    return {"before": np.stack([np.triu(np.ones((P, P), f), 1), np.ones((P, P), f)], 1),
            "steps": (P * np.arange(STEPS)).astype(f), "upto": np.tril(np.ones((E, E), f)).reshape(-1),
            "tile_ids": np.arange(TILES).astype(f), "place0": (REGION * np.arange(E)).astype(f), 
            "dest0": dest0, "blank": blank}


def program(nc, ins, out):
    x1 = nc.dram_tensor("x1_scratch", [B, T, D], F32).ap()
    x_norm = nc.dram_tensor("x_norm_scratch", [B, T, D], F32).ap()
    base = nc.dram_tensor("base_scratch", [B, T, D], F32).ap()
    x_moe = nc.dram_tensor("x_moe_scratch", [B, P, DH, T], F32).ap()
    x_tok = nc.dram_tensor("x_tok_scratch", [B, T, D], F32).ap()
    logits = nc.dram_tensor("logits_scratch", [P, NT * E], F32).ap()
    rows_x = nc.dram_tensor("rows_x_scratch", [ROWS_X, ROW], F32).ap()
    rows_y = nc.dram_tensor("rows_y_scratch", [ROWS_Y, D], F32).ap()
    cross_attention(nc, ins["x"], ins["ctxT"], ins["g_xattn"], ins["wq"], ins["bq"], ins["wk"], ins["bk"],
                    ins["wv"], ins["bv"], ins["wo"], ins["bo"], ins["identity"], ins["key_rows"], x1)
    self_attention(nc, x1, ins["g_ffn"], ins["g1"], ins["wqT"], ins["wkvT"], ins["woT"], ins["g2"],
                   ins["wrT"], ins["identity"], ins["key_rows2"], x_norm, base, x_moe, x_tok, logits)
    experts(nc, x_moe, x_tok, logits, base, ins["g_ffn"], ins["g2"], ins["expert_bias"], ins["w13T"], ins["w2T"],
            ins["iota"], ins["identity"], ins["before"], ins["steps"], ins["upto"], ins["tile_ids"], ins["place0"],
            ins["dest0"], ins["blank"], rows_x, rows_y, out)


def kernel(**inputs):
    import numpy as np
    import concourse.bacc as bacc
    from concourse.bass_utils import run_bass_kernel_spmd

    xa = {k[len("L0_xattn_"):]: np.asarray(v) for k, v in inputs.items() if k.startswith("L0_xattn_")}
    ff = {k[len("L0_ffn_"):]: np.asarray(v) for k, v in inputs.items() if k.startswith("L0_ffn_")}

    def slab_order(w):
        return w.reshape(-1, PACKS, 2, 2, DK).transpose(0, 2, 1, 3, 4).reshape(-1, D)

    def columns(v):
        return v.reshape(DH, P).T

    key_rows = np.zeros((P, 2, T), np.float32)
    for place in range(2):
        key_rows[96 + place, place] = 1
        key_rows[98 + place, place] = 1
    key_rows2 = np.zeros((P, 2, T), np.float32)
    key_rows2[KC:KC + 2, 1] = 1

    arrays = {
        "x": inputs["x"], "ctxT": np.asarray(inputs["ctx_512"]).transpose(0, 2, 1), "g_xattn": inputs["g_xattn"],
        "wq": slab_order(xa["Wq"]), "bq": columns(slab_order(xa["bq"]).reshape(D)),
        "wk": slab_order(xa["Wk"]), "bk": columns(slab_order(xa["bk"]).reshape(D)),
        "wv": xa["Wv"], "bv": xa["bv"], "wo": xa["Wo"], "bo": xa["bo"],
        "g_ffn": inputs["g_ffn"], "g1": columns(ff["g1"]), "g2": columns(ff["g2"]), "wqT": ff["Wq"].T,
        "wkvT": np.concatenate([ff["Wkc"].T, ff["Wvc"].T], 1), "woT": ff["Wo"].T,
        "wrT": ff["Wr"].T, "expert_bias": ff["expert_bias"],
        "w13T": np.concatenate([np.concatenate([ff["sW1"][None], ff["eW1"]]).transpose(0, 2, 1),
                                np.concatenate([ff["sW3"][None], ff["eW3"]]).transpose(0, 2, 1)], 2),
        "w2T": np.concatenate([ff["sW2"][None], ff["eW2"]]).transpose(0, 2, 1),
        "identity": np.eye(P, dtype=np.float32), "key_rows": key_rows, "key_rows2": key_rows2,
        "iota": np.arange(E, dtype=np.float32), **routing_constants(),
    }
    nc = bacc.Bacc("TRN2", target_bir_lowering=False, num_devices=1)
    arrays = {name: np.ascontiguousarray(a) for name, a in arrays.items()}
    ins = {name: nc.dram_tensor(f"in_{name}", a.shape, mybir.dt.from_np(a.dtype), kind="ExternalInput").ap()
           for name, a in arrays.items()}
    out = nc.dram_tensor("out", (B, T, D), F32, kind="ExternalOutput").ap()
    program(nc, ins, out)
    run = run_bass_kernel_spmd(nc, [{f"in_{name}": a for name, a in arrays.items()}], core_ids=[0])
    return run.results[0]["out"]
```
